# Optimizing a Trainium2 kernel written in Bass

```python
import numpy as np
import jax
import jax.numpy as jnp

def _softmax(x, axis=-1):
    return jax.nn.softmax(x, axis=axis)

def _gelu(x):
    return jax.nn.gelu(x, approximate=True)

def _silu(x):
    return jax.nn.silu(x)

def _sigmoid(x):
    return jax.nn.sigmoid(x)

def _layernorm(x, axis=-1, eps=1e-05):
    m = jnp.mean(x, axis=axis, keepdims=True)
    v = jnp.var(x, axis=axis, keepdims=True)
    return (x - m) / jnp.sqrt(v + eps)

def _scatter_add(tgt, idx, src, axis=0):
    return tgt.at[idx].add(src)

def _segment_sum(src, seg, n):
    return jax.ops.segment_sum(src, seg, n)
kernel_name = 'mk_adj_preln_d2_adj_r2_5a6507'

def setup_inputs(seed: int=0):
    np.random.seed(seed)
    _w = jnp.asarray

    def _rec_inputs():
        import jax
        import jax.numpy as jnp
        _gk = jax.random.key(seed)
        x = -0.0005207 + 1.001 * jax.random.normal(jax.random.fold_in(_gk, 1), (16, 512, 256), jnp.float32)
        _a = jax.random.bernoulli(jax.random.fold_in(_gk, 2), 0.03125, (16, 512, 512))
        adj = _a.astype(jnp.int32)
        return (x, adj)
    x, adj = _rec_inputs()

    def _L0_gnn_setup():
        import jax, jax.numpy as jnp
        import numpy as np
        NEG_INF = -1e+30
        NEG_SLOPE = 0.2
        key = jax.random.key(seed)
        k1, k2, k3, k4, k5 = jax.random.split(key, 5)
        B, N, D, H = (2, 1024, 256, 8)
        k = D // H
        return {'x': jax.random.normal(k1, (B, N, D), dtype=jnp.float32), 'A': jax.random.randint(k2, (B, N, N), 0, 2, dtype=jnp.int32), 'W_proj': jax.random.normal(k3, (D, D), dtype=jnp.float32) * (1.0 / np.sqrt(D)), 'W_att': jax.random.normal(k4, (H, 2 * k), dtype=jnp.float32) * (1.0 / np.sqrt(2 * k)), 'b_att': jax.random.normal(k5, (H,), dtype=jnp.float32) * 0.01}
    _L0_gnn_all = _L0_gnn_setup()
    _L0_gnn_in = {k: v for k, v in _L0_gnn_all.items() if k in ('W_proj', 'W_att', 'b_att')}
    del _L0_gnn_all

    def _L1_gnn_setup():
        import jax, jax.numpy as jnp
        import numpy as np
        NEG_INF = -1000000000.0
        NEG_SLOPE = 0.2

        def gat_layer(x, mask, W, a_src, a_dst, bias, concat):
            B, N, _ = x.shape
            H, F = a_src.shape
            xl = (x @ W).reshape(B, N, H, F)
            asrc = jnp.einsum('bnhf,hf->bnh', xl, a_src)
            adst = jnp.einsum('bnhf,hf->bnh', xl, a_dst)
            e = jax.nn.leaky_relu(asrc[:, :, None, :] + adst[:, None, :, :], NEG_SLOPE)
            e = jnp.where(mask[..., None], e, NEG_INF)
            attn = jax.nn.softmax(e, axis=1)
            out = jnp.einsum('bsdh,bshf->bdhf', attn, xl)
            if concat:
                out = out.reshape(B, N, H * F)
            else:
                out = out.mean(axis=2)
            return out + bias
        key = jax.random.key(seed)
        ks = jax.random.split(key, 10)
        B, N, Din, Fh, H, Dout = (8, 512, 256, 128, 4, 256)
        s = 0.05
        return {'adj': jax.random.randint(ks[0], (B, N, N), 0, 2, dtype=jnp.int32), 'x': jax.random.normal(ks[1], (B, N, Din), dtype=jnp.float32), 'W1': jax.random.normal(ks[2], (Din, H * Fh), dtype=jnp.float32) * s, 'att_src1': jax.random.normal(ks[3], (H, Fh), dtype=jnp.float32) * s, 'att_dst1': jax.random.normal(ks[4], (H, Fh), dtype=jnp.float32) * s, 'b1': jax.random.normal(ks[5], (H * Fh,), dtype=jnp.float32) * s, 'W2': jax.random.normal(ks[6], (H * Fh, Dout), dtype=jnp.float32) * s, 'att_src2': jax.random.normal(ks[7], (1, Dout), dtype=jnp.float32) * s, 'att_dst2': jax.random.normal(ks[8], (1, Dout), dtype=jnp.float32) * s, 'b2': jax.random.normal(ks[9], (Dout,), dtype=jnp.float32) * s}
    _L1_gnn_all = _L1_gnn_setup()
    _L1_gnn_in = {k: v for k, v in _L1_gnn_all.items() if k in ('W1', 'att_src1', 'att_dst1', 'b1', 'W2', 'att_src2', 'att_dst2', 'b2')}
    del _L1_gnn_all
    return {'x': x, 'adj': adj, 'L0_gnn_W_proj': _L0_gnn_in['W_proj'], 'L0_gnn_W_att': _L0_gnn_in['W_att'], 'L0_gnn_b_att': _L0_gnn_in['b_att'], 'L1_gnn_W1': _L1_gnn_in['W1'], 'L1_gnn_att_src1': _L1_gnn_in['att_src1'], 'L1_gnn_att_dst1': _L1_gnn_in['att_dst1'], 'L1_gnn_b1': _L1_gnn_in['b1'], 'L1_gnn_W2': _L1_gnn_in['W2'], 'L1_gnn_att_src2': _L1_gnn_in['att_src2'], 'L1_gnn_att_dst2': _L1_gnn_in['att_dst2'], 'L1_gnn_b2': _L1_gnn_in['b2']}

def reference(x, adj, L0_gnn_W_proj, L0_gnn_W_att, L0_gnn_b_att, L1_gnn_W1, L1_gnn_att_src1, L1_gnn_att_dst1, L1_gnn_b1, L1_gnn_W2, L1_gnn_att_src2, L1_gnn_att_dst2, L1_gnn_b2):
    import jax
    import jax.numpy as jnp

    def _L0_gnn_ref(x, A, W_proj, W_att, b_att):
        import jax, jax.numpy as jnp
        import numpy as np
        NEG_INF = -1e+30
        NEG_SLOPE = 0.2
        B, N, _ = x.shape
        H, two_k = W_att.shape
        k = two_k // 2
        xp = jnp.einsum('bnd,do->bno', x, W_proj)
        xh = xp.reshape(B, N, H, k).transpose(0, 2, 1, 3)
        a_src = jnp.einsum('bhnk,hk->bhn', xh, W_att[:, :k])
        a_dst = jnp.einsum('bhnk,hk->bhn', xh, W_att[:, k:])
        scores = a_src[:, :, :, None] + a_dst[:, :, None, :] + b_att[None, :, None, None]
        scores = jax.nn.leaky_relu(scores, negative_slope=NEG_SLOPE)
        mask = (A > 0)[:, None, :, :]
        scores = jnp.where(mask, scores, NEG_INF)
        att = jax.nn.softmax(scores, axis=-1)
        out = jax.nn.relu(jnp.einsum('bhij,bhjk->bhik', att, xh))
        return out.transpose(0, 2, 1, 3).reshape(B, N, H * k)

    def _L1_gnn_ref(adj, x, W1, att_src1, att_dst1, b1, W2, att_src2, att_dst2, b2):
        import jax, jax.numpy as jnp
        import numpy as np
        NEG_INF = -1000000000.0
        NEG_SLOPE = 0.2

        def gat_layer(x, mask, W, a_src, a_dst, bias, concat):
            B, N, _ = x.shape
            H, F = a_src.shape
            xl = (x @ W).reshape(B, N, H, F)
            asrc = jnp.einsum('bnhf,hf->bnh', xl, a_src)
            adst = jnp.einsum('bnhf,hf->bnh', xl, a_dst)
            e = jax.nn.leaky_relu(asrc[:, :, None, :] + adst[:, None, :, :], NEG_SLOPE)
            e = jnp.where(mask[..., None], e, NEG_INF)
            attn = jax.nn.softmax(e, axis=1)
            out = jnp.einsum('bsdh,bshf->bdhf', attn, xl)
            if concat:
                out = out.reshape(B, N, H * F)
            else:
                out = out.mean(axis=2)
            return out + bias
        B, N, _ = adj.shape
        mask = (adj > 0) | jnp.eye(N, dtype=bool)[None]
        h = jax.nn.elu(gat_layer(x, mask, W1, att_src1, att_dst1, b1, concat=True))
        h = gat_layer(h, mask, W2, att_src2, att_dst2, b2, concat=False)
        return h
    h = jnp.maximum(_layernorm(x, axis=-1), 0.0)
    x = x + _L0_gnn_ref(h, adj, L0_gnn_W_proj, L0_gnn_W_att, L0_gnn_b_att)
    h = jnp.maximum(_layernorm(x, axis=-1), 0.0)
    x = x + _L1_gnn_ref(adj, h, L1_gnn_W1, L1_gnn_att_src1, L1_gnn_att_dst1, L1_gnn_b1, L1_gnn_W2, L1_gnn_att_src2, L1_gnn_att_dst2, L1_gnn_b2)
    return x

_drawn_inputs = setup_inputs


def setup_inputs(seed=0):
    import zlib

    import numpy as np

    out = dict(_drawn_inputs(seed))
    spreads = {}
    factors = {'L0_gnn_b_att': 64.0,
     'L1_gnn_att_src1': 6.59,
     'L1_gnn_att_dst1': 8.0,
     'L1_gnn_att_src2': 8.0,
     'L1_gnn_att_dst2': 22.726}
    for name, (base, spread) in spreads.items():
        noise = np.random.default_rng([zlib.crc32(name.encode()), seed]).standard_normal(out[name].shape)
        drawn = base * np.exp(spread * noise) if base else spread * noise
        out[name] = jnp.asarray(drawn.astype(out[name].dtype))
    for name, factor in factors.items():
        out[name] = (out[name] * factor).astype(out[name].dtype)
    return out
```

```python
from contextlib import ExitStack

import concourse.bass as bass
from concourse import mybir

ALU = mybir.AluOpType
ACT = mybir.ActivationFunctionType
AX_X = mybir.AxisListType.X
F32 = mybir.dt.float32
F32R = mybir.dt.float32r
BF16 = mybir.dt.bfloat16
I32 = mybir.dt.int32

P = 128
LO = 32
SLOPE = 0.2
EPS = 1e-5
LIFT = 60.0
TINY = 1e-37


class Signal:

    def __init__(self, sem, per_batch):
        self.sem, self.per_batch = sem, per_batch

    def after(self, n, k):
        return self.per_batch * n + k


class Bank:

    def __init__(self, tensor, full, free):
        self.t, self.full, self.free = tensor, full, free


def started(n, k=0):
    return not (isinstance(n, int) and n == 0 and k == 0)


def gnn_kernel(nc, x, adj, w_proj, w_att, b_att, w1, att_src1, att_dst1, b1, w2, att_src2, att_dst2, b2, out):
    B, N, D = x.shape
    H0, K2 = w_att.shape
    K0 = K2 // 2
    H1, F1 = att_src1.shape
    F2 = att_src2.shape[1]
    NB = N // P
    KB = D // P
    FB = H1 * F1 // P
    assert F1 == P and H0 * K0 == D and F2 == D and H0 % 4 == 0 and N == 512 and B % 2 == 0

    with ExitStack() as ctx:
        def sb(name, shape, dt=F32):
            return ctx.enter_context(nc.sbuf_tensor(name, shape, dt))

        def signal(name, per_batch=1):
            return Signal(ctx.enter_context(nc.semaphore(name)), per_batch)

        def bank(name, full, free):
            return Bank(ctx.enter_context(nc.psum_tensor(name, [P, 512], F32)),
                        signal(name + "_full", full), signal(name + "_free", free))

        a_m = bank("a_m", 4, 4)
        a_o = [bank("a_o0", 2, 4), bank("a_o1", 2, 4)]
        a_g = bank("a_g", 1 + H0, 1 + H0)
        b_m = bank("b_m", 3 + H1, 3 + H1)
        b_o = [bank("b_o0", 4, 8), bank("b_o1", 5, 9)]
        b_g = bank("b_g", H1 + 1, H1 + 1)

        WP = sb("WP", [P, KB, D])
        W1 = sb("W1", [P, KB, H1 * F1])
        W2 = sb("W2", [P, FB, F2])
        att0 = sb("att0", [P, H0, K2])
        att1 = sb("att1", [P, 2, H1, F1])
        att2 = sb("att2", [P, 2, F2])
        prod = sb("prod", [P, H1 * F1])
        rows_w = {"a": sb("rows_w0", [P, KB, LO + H0]), "b": sb("rows_w1", [P, KB, LO + H1]),
                  "c": sb("rows_w2", [P, FB, LO + 1])}
        batt = sb("batt", [H0, 1])
        b1c = sb("b1c", [P, H1])
        b2r = sb("b2r", [P, F2])
        ident = sb("ident", [P, P])
        identb = sb("identb", [P, P], BF16)
        pick32 = sb("pick32", [LO + H0, H0, P])
        pick = sb("pick", [LO + H0, H0, P], F32R)
        lift = sb("lift", [P, 1])
        one = sb("one", [P, 1])
        b1n = sb("b1n", [P, H1])
        power = sb("power", [P, NB])

        X = [sb(f"X{p}", [P, NB, D]) for p in range(2)]
        ADJ = sb("ADJ", [P, NB, N], I32)
        MASK = [sb(f"MASK{p}", [P, NB, N], BF16) for p in range(2)]
        MASKT = sb("MASKT", [P, NB, N], BF16)
        X1 = [sb(f"X1{p}", [P, NB, D]) for p in range(2)]
        X1B = sb("X1B", [P, NB, D])
        XM = sb("XM", [P, NB, D])
        T = sb("T", [P, H0 // 2, NB, 2 * K0])
        OUT = sb("OUT", [P, NB, F2])
        RM = sb("RM", [P, D])
        hsum = sb("hsum", [P, KB])
        none = sb("none", [P, NB])
        stats = {t: sb("stats_" + t, [P, NB, 6]) for t in "ab"}
        mv = {t: sb("mv_" + t, [P, NB, 5]) for t in "ab"}
        veps = {t: sb("veps_" + t, [P, NB]) for t in "ab"}
        rstd = {t: sb("rstd_" + t, [P, NB]) for t in "ab"}
        shift = {t: sb("shift_" + t, [P, NB]) for t in "ab"}
        Hn = {t: sb("H_" + t, [P, NB, D]) for t in "ab"}
        HT = {t: sb("HT_" + t, [P, KB, N]) for t in "ab"}
        GT = sb("GT", [P, FB, N])
        heads = {"a": H0, "b": H1, "c": 1}
        top = {t: sb("top_" + t, [LO + H0, 1]) for t in "abc"}
        atop = {t: sb("atop_" + t, [H0, 1]) for t in "abc"}
        top8 = {t: sb("top8_" + t, [LO + H0, 1]) for t in "abc"}
        top2 = {t: sb("top2_" + t, [LO + H0, 1]) for t in "abc"}
        top2lo = {t: sb("top2lo_" + t, [H0, 1]) for t in "abc"}
        Z = {t: sb("Z_" + t, [H0, N]) for t in "abc"}
        G = {t: sb("G_" + t, [H0, N]) for t in "abc"}
        GS = {t: sb("GS_" + t, [LO + heads[t], N], F32R) for t in "abc"}
        RT = {t: sb("RT_" + t, [P, N]) for t in "abc"}
        SC = {t: sb("SC_" + t, [P, NB, LO + heads[t]]) for t in "abc"}
        V0 = sb("V0", [P, NB, H0, K0 + 1])
        V1 = sb("V1", [P, NB, H1, F1 + 1])
        V2 = sb("V2", [P, NB, F2 + 1])
        GB = {t: [sb(f"GB_{t}{q}", [P, N]) for q in range(2)] for t in "ab"}
        W = {t: [sb(f"W_{t}{q}", [P, NB, N]) for q in range(2)] for t in "ab"}
        den = {t: sb("den_" + t, [P, 8]) for t in "ab"}
        rden = {t: sb("rden_" + t, [P, 8]) for t in "ab"}
        Y = sb("Y", [P, NB, F1])
        EX = sb("EX", [P, N])
        EM = sb("EM", [P, N])
        RL = sb("RL", [P, N])
        NR = sb("NR", [P, N])

        w_in = signal("w_in")
        cst = signal("cst")
        cst_b = signal("cst_b")
        setup = signal("setup")
        x_in = [signal(f"x_in{p}", 8) for p in range(2)]
        adj_in = signal("adj_in", 16)
        s_bn = {t: signal("bn_" + t, NB) for t in "ab"}
        s_mv = {t: signal("mv_done_" + t, 5) for t in "ab"}
        s_ve = {t: signal("veps_done_" + t) for t in "ab"}
        s_rstd = {t: signal("rstd_done_" + t) for t in "ab"}
        s_shift = {t: signal("shift_done_" + t) for t in "ab"}
        s_h = {t: signal("h_done_" + t, NB) for t in "ab"}
        s_top = {t: signal("top_done_" + t) for t in "abc"}
        s_small = {t: signal("small_done_" + t, 4) for t in "abc"}
        s_z = {t: signal("z_done_" + t) for t in "abc"}
        s_g = {t: signal("g_done_" + t) for t in "abc"}
        s_gh = {t: signal("g_high_" + t) for t in "abc"}
        s_gl = {t: signal("g_low_" + t) for t in "abc"}
        s_den = {t: signal("den_col_" + t) for t in "abc"}
        s_mask = signal("mask_done")
        s_diag = signal("diag_done", 2)
        s_w = {"a": signal("weights_a", H0), "b": signal("weights_b", H1 + 1)}
        s_pv = {"a": signal("sums_a", H0), "b": signal("sums_b", H1 + 1)}
        s_half = signal("half_sums_b", H1 + NB - 1)
        s_den_r = {"a": signal("den_a", H0 // 2), "b": signal("den_b", 2 * H1 + NB)}
        s_rden = {"a": signal("rden_a", H0 // 2), "b": signal("rden_b", 2 * H1 + NB)}
        s_none = signal("none_done")
        s_xm = signal("xm_done", NB)
        s_x1 = signal("x1_done", H0 // 2)
        s_ex = signal("exp_done", H1)
        s_em = signal("em_done", H1)
        s_gt = signal("gt_done", H1)
        s_x1b = signal("x1b_done")
        s_fin = signal("fin_done", NB)
        s_out = signal("out_done", 16)

        N_W = 16 * 11

        block = ctx.enter_context(nc.Block())

        @block.sync
        def _(sp):
            def load(n, p):
                if started(n) and not (isinstance(n, int) and n < 2):
                    sp.wait_ge(s_xm.sem, s_xm.after(n - 2, NB))
                sp.dma_start(X[p][:], x[n].rearrange("(b p) d -> p b d", p=P)).then_inc(x_in[p].sem, 16)
                if started(n):
                    sp.wait_ge(s_mask.sem, s_mask.after(n - 1, 1))
                sp.dma_start(ADJ[:], adj[n].rearrange("(b p) j -> p b j", p=P)).then_inc(adj_in.sem, 16)

            def store(n):
                sp.wait_ge(s_fin.sem, s_fin.after(n, NB))
                sp.dma_start(out[n].rearrange("(b p) d -> p b d", p=P), OUT[:]).then_inc(s_out.sem, 16)

            load(0, 0)
            for dst, src in (
                (WP[:], w_proj.rearrange("(k p) o -> p k o", p=P)),
                (W1[:], w1.rearrange("(k p) o -> p k o", p=P)),
                (W2[:], w2.rearrange("(k p) o -> p k o", p=P)),
                (att0[:], w_att.partition_broadcast(P)),
                (att1[:, 0], att_dst1.partition_broadcast(P)),
                (att1[:, 1], att_src1.partition_broadcast(P)),
                (att2[:, 0], att_dst2[0].partition_broadcast(P)),
                (att2[:, 1], att_src2[0].partition_broadcast(P)),
                (b2r[:], b2.partition_broadcast(P)),
                (batt[:], b_att.rearrange("(h a) -> h a", a=1)),
                (b1c[:], b1.rearrange("(h p) -> p h", p=P)),
            ):
                with nc.allow_non_contiguous_dma(reason="two short vectors, once"):
                    sp.dma_start(dst, src).then_inc(w_in.sem, 16)
            load(1, 1)
            with sp.Fori(0, B // 2 - 1) as i:
                for p in range(2):
                    load(2 * i + 2 + p, p)
                    store(2 * i + p)
            store(B - 2)
            store(B - 1)
            sp.wait_ge(s_out.sem, s_out.after(B - 1, 16))

        def joints(engine, joint):
            joint(None, None, 0, 0)
            joint(0, 0, 1, 1)
            with engine.Fori(0, B // 2 - 1) as i:
                joint(2 * i + 1, 1, 2 * i + 2, 0)
                joint(2 * i + 2, 0, 2 * i + 3, 1)
            joint(B - 1, (B - 1) % 2, None, None)

        @block.gpsimd
        def _(pool):
            pool.memset(ident[:], 0.0).then_inc(cst.sem, 1)
            pool.memset(pick32[:], 0.0).then_inc(cst.sem, 1)
            pool.memset(lift[:], LIFT).then_inc(cst.sem, 1)
            pool.memset(power[:], -0.5).then_inc(cst.sem, 1)
            pool.memset(one[:], 1.0).then_inc(cst.sem, 1)
            pool.wait_ge(cst.sem, 5)
            pool.affine_select(out=ident[:], in_=ident[:], compare_op=ALU.not_equal, fill=1.0, base=0,
                               pattern=[[-1, P]], channel_multiplier=1).then_inc(cst.sem, 1)
            pool.affine_select(out=pick32[:], in_=pick32[:], compare_op=ALU.not_equal, fill=1.0, base=0,
                               pattern=[[-1, H0], [0, P]], channel_multiplier=1).then_inc(cst.sem, 1)
            pool.wait_ge(cst.sem, 7)
            pool.affine_select(out=pick32[:], in_=pick32[:], compare_op=ALU.not_equal, fill=1.0, base=-LO,
                               pattern=[[-1, H0], [0, P]], channel_multiplier=1).then_inc(cst.sem, 1)
            pool.tensor_copy(identb[:], ident[:]).then_inc(cst.sem, 1)
            for t in "abc":
                pool.memset(RT[t][:], 0.0).then_inc(cst.sem, 1)
            pool.wait_ge(cst.sem, 12)

            def rstd_of(t, n):
                pool.wait_ge(s_ve[t].sem, s_ve[t].after(n, 1))
                pool.tensor_tensor(rstd[t][:], veps[t][:], power[:], ALU.pow).then_inc(s_rstd[t].sem, 1)

            def elu(n, h):
                pool.wait_ge(s_ex.sem, s_ex.after(n, h + 1))
                pool.tensor_tensor(EM[:], EX[:], one[:].to_broadcast([P, N]), ALU.subtract).then_inc(s_em.sem, 1)
                pool.wait_ge(s_em.sem, s_em.after(n, h + 1))
                pool.tensor_tensor(GT[:, h, :], EM[:], RL[:], ALU.add).then_inc(s_gt.sem, 1)

            def x1(n, p, g):
                if g == 0:
                    pool.wait_ge(s_xm.sem, s_xm.after(n, NB))
                else:
                    pool.wait_ge(a_o[g % 2].free.sem, a_o[g % 2].free.after(n, 3 + g // 2))
                c = slice(2 * K0 * g, 2 * K0 * (g + 1))
                pool.tensor_tensor(X1[p][:, :, c], T[:, g], XM[:, :, c], ALU.add).then_inc(s_x1.sem, 1)

            def x1b(n, p):
                if started(n):
                    pool.wait_ge(s_fin.sem, s_fin.after(n - 1, NB))
                pool.tensor_tensor(X1B[:], X1[p][:], b2r[:].unsqueeze(1).to_broadcast([P, NB, F2]),
                                   ALU.add).then_inc(s_x1b.sem, 1)

            def joint(nb, pb, na, pa):
                if na is not None:
                    rstd_of("a", na)
                if nb is not None:
                    x1b(nb, pb)
                    elu(nb, 0)
                if na is not None:
                    x1(na, pa, 0)
                if nb is not None:
                    elu(nb, 1)
                    elu(nb, 2)
                if na is not None:
                    x1(na, pa, 1)
                if nb is not None:
                    elu(nb, 3)
                if na is not None:
                    x1(na, pa, 2)
                    x1(na, pa, 3)
                    rstd_of("b", na)

            pool.wait_ge(w_in.sem, N_W)
            joints(pool, joint)

        @block.scalar
        def _(act):
            act.wait_ge(cst.sem, 12)
            act.wait_ge(w_in.sem, N_W)
            act.wait_ge(cst_b.sem, 2)

            def normalize(t, n, src):
                act.wait_ge(s_shift[t].sem, s_shift[t].after(n, 1))
                for b in range(NB):
                    act.activation(Hn[t][:, b, :], src[:, b, :], ACT.Relu, bias=shift[t][:, b:b + 1],
                                   scale=rstd[t][:, b:b + 1]).then_inc(s_h[t].sem, 1)

            def h_transposed(t, n, banks):
                for k, bk in enumerate(banks):
                    act.wait_ge(bk.full.sem, bk.full.after(n, 1))
                    act.activation(HT[t][:, k, :], bk.t[:], ACT.Copy,
                                   accum_out=hsum[:, k:k + 1] if t == "a" else None).then_inc(bk.free.sem, 1)

            def row_exps(t, n, bk, use):
                nh = heads[t]
                act.wait_ge(s_small[t].sem, s_small[t].after(n, 4))
                act.activation(RT[t][LO:LO + nh, :], bk.t[LO:LO + nh, :], ACT.Exp, bias=top8[t][LO:LO + nh, :],
                               scale=1.0 - SLOPE)
                act.wait_ge(s_z[t].sem, s_z[t].after(n, 1))
                act.activation(RT[t][0:nh, :], bk.t[LO:LO + nh, :], ACT.Exp, bias=top2[t][LO:LO + nh, :],
                               scale=SLOPE).then_inc(bk.free.sem, 1)
                act.activation(G[t][0:nh, :], Z[t][0:nh, :], ACT.Exp, bias=lift[0:nh, :],
                               scale=SLOPE - 1.0).then_inc(s_g[t].sem, 1)
                act.wait_ge(s_g[t].sem, s_g[t].after(n, 1))
                act.activation(GS[t][0:nh, :], G[t][0:nh, :], ACT.Copy).then_inc(s_gh[t].sem, 1)

            def mask_transposed(n):
                if started(n):
                    act.wait_ge(s_w["a"].sem, s_w["a"].after(n - 1, H0))
                for half, (bk, use) in enumerate(((a_m, 2), (a_g, 1))):
                    act.wait_ge(bk.full.sem, bk.full.after(n, use))
                    act.activation(MASKT[:, 2 * half:2 * half + 2, :],
                                   bk.t[:].bitcast(BF16).rearrange("p (b i) -> p b i", b=2),
                                   ACT.Copy).then_inc(bk.free.sem, 1)

            def mean_row(n):
                act.wait_ge(a_m.full.sem, a_m.full.after(n, 4))
                act.activation(RM[:], a_m.t[:, 0:D], ACT.Relu, scale=1.0 / N).then_inc(a_m.free.sem, 1)

            def gates(t, n, h, q, bk, per, first):
                act.wait_ge(bk.full.sem, bk.full.after(n, first + h + 1))
                if not (isinstance(n, int) and n == 0 and h < 2):
                    act.wait_ge(s_w[t].sem, s_w[t].after(n, h - 1))
                act.activation(GB[t][q][:], bk.t[:], ACT.Copy).then_inc(bk.free.sem, 1)

            def gates_a(n, h):
                gates("a", n, h, h % 2, a_g, H0, 1)

            def gates_b(n, p, h):
                gates("b", n, h, (p + h) % 2, b_g, H1 + 1, 0)

            def elu_parts(n, h):
                act.wait_ge(b_m.full.sem, b_m.full.after(n, 3 + h))
                if started(n, h):
                    act.wait_ge(s_gt.sem, s_gt.after(n, h))
                act.activation(RL[:], b_m.t[:], ACT.Relu, bias=b1c[:, h:h + 1])
                act.activation(NR[:], b_m.t[:], ACT.Relu, bias=b1n[:, h:h + 1], scale=-1.0).then_inc(b_m.free.sem, 1)
                act.wait_ge(b_m.free.sem, b_m.free.after(n, 3 + h))
                act.activation(EX[:], NR[:], ACT.Exp, scale=-1.0).then_inc(s_ex.sem, 1)

            def values2(n, half):
                bk = b_o[half]
                act.wait_ge(s_den["c"].sem, s_den["c"].after(n, 1))
                act.wait_ge(bk.full.sem, bk.full.after(n, 4 + half))
                for j in range(2):
                    b = 2 * half + j
                    ins = act.activation(V2[:, b, 0:F2], bk.t[:, j * F2:(j + 1) * F2], ACT.Copy,
                                         scale=SC["c"][:, b, 0:1])
                ins.then_inc(bk.free.sem, 1)

            def joint(nb, pb, na, pa):
                A, Bt = na is not None, nb is not None
                if Bt:
                    h_transposed("b", nb, (b_m, b_o[0]))
                if A:
                    act.wait_ge(x_in[pa].sem, x_in[pa].after(na, 16 - 8 * pa))
                    normalize("a", na, X[pa])
                    h_transposed("a", na, (a_m, a_o[0]))
                if Bt:
                    row_exps("b", nb, b_o[1], 1)
                if A:
                    row_exps("a", na, a_o[1], 1)
                    mask_transposed(na)
                    mean_row(na)
                if Bt:
                    gates_b(nb, pb, 0)
                if A:
                    gates_a(na, 0)
                for h in range(H1):
                    if Bt and h + 1 < H1:
                        gates_b(nb, pb, h + 1)
                    if Bt and h >= 1:
                        elu_parts(nb, h - 1)
                    if A:
                        gates_a(na, h + 1)
                if A:
                    gates_a(na, 5)
                if Bt:
                    elu_parts(nb, 3)
                if A:
                    gates_a(na, 6)
                if Bt:
                    row_exps("c", nb, b_o[1], 8)
                if A:
                    gates_a(na, 7)
                if Bt:
                    values2(nb, 0)
                    values2(nb, 1)
                    gates_b(nb, pb, H1)
                if A:
                    normalize("b", na, X1[pa])

            joints(act, joint)

        @block.vector
        def _(dve):
            dve.memset(rows_w["a"][:], 0.0).then_inc(setup.sem, 1)
            dve.memset(rows_w["b"][:], 0.0).then_inc(setup.sem, 1)
            dve.memset(rows_w["c"][:], 0.0).then_inc(setup.sem, 1)
            for t in "abc":
                dve.memset(GS[t][:].bitcast(F32), 0.0).then_inc(setup.sem, 1)
            done = 6
            dve.wait_ge(w_in.sem, N_W)
            dve.wait_ge(setup.sem, done)
            folds = []
            for k in range(KB):
                for s in range(2):
                    folds.append((WP[:, k, :].rearrange("p (h c) -> p h c", h=H0), att0[:, :, s * K0:(s + 1) * K0],
                                  rows_w["a"][:, k, s * LO:s * LO + H0], H0, K0))
                    folds.append((W1[:, k, :].rearrange("p (h c) -> p h c", h=H1), att1[:, s],
                                  rows_w["b"][:, k, s * LO:s * LO + H1], H1, F1))
            for k in range(FB):
                for s in range(2):
                    folds.append((W2[:, k:k + 1, :], att2[:, s:s + 1, :], rows_w["c"][:, k, s * LO:s * LO + 1], 1, F2))
            for w, att, dst, nh, c in folds:
                pr = prod[:, 0:nh * c].rearrange("p (h c) -> p h c", h=nh)
                dve.tensor_tensor(pr, w, att, ALU.mult).then_inc(setup.sem, 1)
                done += 1
                dve.wait_ge(setup.sem, done)
                dve.tensor_reduce(dst, pr, AX_X, ALU.add).then_inc(setup.sem, 1)
                done += 1
                dve.wait_ge(setup.sem, done)
            dve.wait_ge(cst.sem, 12)
            dve.tensor_copy(pick[:], pick32[:]).then_inc(cst_b.sem, 1)
            dve.tensor_scalar(b1n[:], b1c[:], -1.0, None, ALU.mult).then_inc(cst_b.sem, 1)

            def statistics(t, n, src):
                for b in range(NB):
                    dve.bn_stats(stats[t][:, b, :], src[:, b, :]).then_inc(s_bn[t].sem, 1)
                dve.wait_ge(s_bn[t].sem, s_bn[t].after(n, NB))
                even, odd = stats[t][:, :, 0:3], stats[t][:, :, 3:6]
                dve.tensor_tensor(mv[t][:, :, 0], even[:, :, 1], odd[:, :, 1], ALU.add).then_inc(s_mv[t].sem, 1)
                dve.tensor_tensor(mv[t][:, :, 1], even[:, :, 1], odd[:, :, 1], ALU.subtract).then_inc(s_mv[t].sem, 1)
                dve.tensor_tensor(mv[t][:, :, 2], even[:, :, 2], odd[:, :, 2], ALU.add).then_inc(s_mv[t].sem, 1)
                dve.wait_ge(s_mv[t].sem, s_mv[t].after(n, 3))
                dve.scalar_tensor_tensor(mv[t][:, :, 3], mv[t][:, :, 1], 0.25, mv[t][:, :, 1], ALU.mult,
                                         ALU.mult).then_inc(s_mv[t].sem, 1)
                dve.tensor_scalar(mv[t][:, :, 4], mv[t][:, :, 2], 1.0 / D, EPS, ALU.mult,
                                  ALU.add).then_inc(s_mv[t].sem, 1)
                dve.wait_ge(s_mv[t].sem, s_mv[t].after(n, 5))
                if started(n):
                    dve.wait_ge(s_h[t].sem, s_h[t].after(n - 1, NB))
                dve.tensor_tensor(veps[t][:], mv[t][:, :, 3], mv[t][:, :, 4], ALU.add).then_inc(s_ve[t].sem, 1)

            def mean_shift(t, n):
                dve.wait_ge(s_rstd[t].sem, s_rstd[t].after(n, 1))
                dve.scalar_tensor_tensor(shift[t][:], mv[t][:, :, 0], -0.5, rstd[t][:], ALU.mult,
                                         ALU.mult).then_inc(s_shift[t].sem, 1)

            def bounds(t, n, bk, use):
                nh = heads[t]
                dve.wait_ge(bk.full.sem, bk.full.after(n, use))
                dve.tensor_reduce(top[t][LO:LO + nh, :], bk.t[LO:LO + nh, :], AX_X, ALU.max).then_inc(s_top[t].sem, 1)
                dve.wait_ge(s_top[t].sem, s_top[t].after(n, 1))
                if t == "a":
                    dve.tensor_copy(top2lo[t][0:nh, :], top[t][LO:LO + nh, :]).then_inc(s_small[t].sem, 1)
                    dve.wait_ge(s_small[t].sem, s_small[t].after(n, 1))
                    dve.tensor_tensor(atop[t][0:nh, :], top2lo[t][0:nh, :], batt[:], ALU.add).then_inc(s_small[t].sem, 1)
                else:
                    dve.tensor_copy(atop[t][0:nh, :], top[t][LO:LO + nh, :]).then_inc(s_small[t].sem, 2)
                dve.tensor_scalar(top8[t][LO:LO + nh, :], top[t][LO:LO + nh, :], SLOPE - 1.0, LIFT, ALU.mult,
                                  ALU.add).then_inc(s_small[t].sem, 1)
                dve.tensor_scalar(top2[t][LO:LO + nh, :], top[t][LO:LO + nh, :], -SLOPE, None,
                                  ALU.mult).then_inc(s_small[t].sem, 1)
                dve.wait_ge(s_small[t].sem, s_small[t].after(n, 4))
                dve.tensor_scalar(Z[t][0:nh, :], bk.t[0:nh, :], atop[t][0:nh, :], 0.0, ALU.add,
                                  ALU.max).then_inc(s_z[t].sem, 1)

            def gate_low(t, n):
                nh = heads[t]
                dve.wait_ge(s_gh[t].sem, s_gh[t].after(n, 1))
                dve.tensor_tensor(GS[t][LO:LO + nh, :], G[t][0:nh, :], GS[t][0:nh, :].bitcast(F32),
                                  ALU.subtract).then_inc(s_gl[t].sem, 1)

            def scalars(t, n, bk, use, dst):
                w = LO + heads[t]
                dve.wait_ge(bk.full.sem, bk.full.after(n, use))
                dve.tensor_copy(SC[t][:], bk.t[:].rearrange("p (b w) -> p b w", b=NB)[:, :, 0:w]).then_inc(bk.free.sem, 1)
                dve.wait_ge(bk.free.sem, bk.free.after(n, use))
                dve.tensor_copy(dst, SC[t][:, :, 0:heads[t]]).then_inc(s_den[t].sem, 1)

            def values0(n, half):
                bk = a_o[half]
                dve.wait_ge(bk.full.sem, bk.full.after(n, 2))
                for j in range(2):
                    b = 2 * half + j
                    ins = dve.tensor_tensor(V0[:, b, :, 0:K0],
                                            bk.t[:, j * D:(j + 1) * D].rearrange("p (h c) -> p h c", h=H0),
                                            SC["a"][:, b, 0:H0].unsqueeze(2).to_broadcast([P, H0, K0]), ALU.mult)
                ins.then_inc(bk.free.sem, 1)

            def values1(n, b):
                bk = b_o[b % 2]
                dve.wait_ge(bk.full.sem, bk.full.after(n, 2 + b // 2))
                dve.tensor_tensor(V1[:, b, :, 0:F1], bk.t[:].rearrange("p (h c) -> p h c", h=H1),
                                  SC["b"][:, b, 0:H1].unsqueeze(2).to_broadcast([P, H1, F1]),
                                  ALU.mult).then_inc(bk.free.sem, 1)

            def weights(t, s, n, h, q, bk, first, hh, mask):
                dve.wait_ge(bk.free.sem, bk.free.after(n, first + h + 1))
                if not (isinstance(n, int) and n == 0 and h < 2):
                    dve.wait_ge(s_pv[t].sem, s_pv[t].after(n, h - 1))
                for b in range(NB):
                    ins = dve.scalar_tensor_tensor(W[t][q][:, b, :], GB[t][q][:], SC[s][:, b, LO + hh:LO + hh + 1],
                                                   mask[:, b, :], ALU.max, ALU.mult)
                ins.then_inc(s_w[t].sem, 1)

            def weights_a(n, h):
                if h == 0:
                    dve.wait_ge(a_m.free.sem, a_m.free.after(n, 2))
                    dve.wait_ge(a_g.free.sem, a_g.free.after(n, 1))
                weights("a", "a", n, h, h % 2, a_g, 1, h, MASKT)

            def weights_b(n, p, h):
                if h == 0:
                    dve.wait_ge(s_diag.sem, s_diag.after(n, 2))
                s, hh = ("b", h) if h < H1 else ("c", 0)
                weights("b", s, n, h, (p + h) % 2, b_g, 0, hh, MASK[p])

            def inverse(t, n, k, src, w):
                dve.tensor_scalar(den[t][:, 0:w], src, TINY, None, ALU.max).then_inc(s_den_r[t].sem, 1)
                dve.wait_ge(s_den_r[t].sem, s_den_r[t].after(n, k))
                dve.reciprocal(rden[t][:, 0:w], den[t][:, 0:w]).then_inc(s_rden[t].sem, 1)
                dve.wait_ge(s_rden[t].sem, s_rden[t].after(n, k))

            def outputs0(n, p, g):
                bk = a_o[g % 2]
                dve.wait_ge(s_pv["a"].sem, s_pv["a"].after(n, 2 * g + 2))
                sums = bk.t[:, 0:2 * NB * (K0 + 1)].rearrange("p (g c) -> p g c", c=K0 + 1)
                inverse("a", n, g + 1, sums[:, :, K0], 2 * NB)
                if g == 0:
                    dve.tensor_scalar(none[:], den["a"][:].rearrange("p (b h) -> p b h", h=2)[:, :, 0], TINY, None,
                                      ALU.is_le).then_inc(s_none.sem, 1)
                dve.scalar_tensor_tensor(T[:, g].rearrange("p b (h c) -> p (b h) c", h=2), sums[:, :, 0:K0], 0.0,
                                         rden["a"][:].unsqueeze(2).to_broadcast([P, 2 * NB, K0]), ALU.max,
                                         ALU.mult).then_inc(bk.free.sem, 1)
                if g == 0:
                    dve.wait_ge(s_none.sem, s_none.after(n, 1))
                    dve.wait_ge(a_m.free.sem, a_m.free.after(n, 4))
                    for b in range(NB):
                        dve.scalar_tensor_tensor(XM[:, b, :], RM[:], none[:, b:b + 1], X[p][:, b, :], ALU.mult,
                                                 ALU.add).then_inc(s_xm.sem, 1)

            def outputs1(n, h):
                for half in range(2):
                    bk = b_o[half]
                    if half == 0:
                        dve.wait_ge(s_half.sem, s_half.after(n, h + 1))
                    else:
                        dve.wait_ge(s_pv["b"].sem, s_pv["b"].after(n, h + 1))
                    sums = bk.t[:, 0:2 * (F1 + 1)].rearrange("p (b c) -> p b c", c=F1 + 1)
                    inverse("b", n, 2 * h + half + 1, sums[:, :, F1], 2)
                    if h:
                        dve.wait_ge(b_m.full.sem, b_m.full.after(n, 2 + h))
                    dve.tensor_tensor(Y[:, 2 * half:2 * half + 2, :], sums[:, :, 0:F1],
                                      rden["b"][:, 0:2].unsqueeze(2).to_broadcast([P, 2, F1]),
                                      ALU.mult).then_inc(bk.free.sem, 1)

            def final(n):
                dve.wait_ge(s_x1b.sem, s_x1b.after(n, 1))
                if started(n):
                    dve.wait_ge(s_out.sem, s_out.after(n - 1, 16))
                for b in range(NB):
                    bk = b_o[b % 2]
                    if b < NB - 1:
                        dve.wait_ge(s_half.sem, s_half.after(n, H1 + b + 1))
                    else:
                        dve.wait_ge(s_pv["b"].sem, s_pv["b"].after(n, H1 + 1))
                    inverse("b", n, 2 * H1 + b + 1, bk.t[:, F2:F2 + 1], 1)
                    dve.scalar_tensor_tensor(OUT[:, b, :], bk.t[:, 0:F2], rden["b"][:, 0:1], X1B[:, b, :], ALU.mult,
                                             ALU.add).then_inc(s_fin.sem, 1)

            def mask(n, p):
                dve.wait_ge(adj_in.sem, adj_in.after(n, 16))
                dve.tensor_scalar(MASK[p][:], ADJ[:], 0.0, None, ALU.is_gt).then_inc(s_mask.sem, 1)

            def diagonal(n, p):
                dve.wait_ge(a_g.full.sem, a_g.full.after(n, 1))
                flat = MASK[p][:].rearrange("p b j -> p (b j)")
                step = N + P
                head = flat[:, 0:(NB - 1) * step].rearrange("p (b c) -> p b c", c=step)[:, :, 0:P]
                tail = flat[:, (NB - 1) * step:NB * N]
                dve.tensor_tensor(head, head, identb[:].unsqueeze(1).to_broadcast([P, NB - 1, P]),
                                  ALU.max).then_inc(s_diag.sem, 1)
                dve.tensor_tensor(tail, tail, identb[:], ALU.max).then_inc(s_diag.sem, 1)

            def joint(nb, pb, na, pa):
                A, Bt = na is not None, nb is not None
                if A:
                    dve.wait_ge(x_in[pa].sem, x_in[pa].after(na, 16 - 8 * pa))
                    statistics("a", na, X[pa])
                    mean_shift("a", na)
                    mask(na, pa)
                if Bt:
                    bounds("b", nb, b_o[1], 1)
                if A:
                    bounds("a", na, a_o[1], 1)
                if Bt:
                    gate_low("b", nb)
                if A:
                    gate_low("a", na)
                if Bt:
                    scalars("b", nb, b_m, 2, V1[:, :, :, F1])
                if A:
                    diagonal(na, pa)
                    scalars("a", na, a_m, 3, V0[:, :, :, K0])
                if Bt:
                    values1(nb, 0)
                if A:
                    values0(na, 0)
                    values0(na, 1)
                if Bt:
                    for b in range(1, NB):
                        values1(nb, b)
                for h in range(H1):
                    if Bt:
                        weights_b(nb, pb, h)
                        if h:
                            outputs1(nb, h - 1)
                    if A:
                        if h == 2:
                            outputs0(na, pa, 0)
                        weights_a(na, h)
                if Bt:
                    outputs1(nb, H1 - 1)
                if A:
                    weights_a(na, 4)
                    outputs0(na, pa, 1)
                    weights_a(na, 5)
                if Bt:
                    bounds("c", nb, b_o[1], 4)
                if A:
                    weights_a(na, 6)
                if Bt:
                    gate_low("c", nb)
                    scalars("c", nb, b_m, 7, V2[:, :, F2:F2 + 1])
                if A:
                    outputs0(na, pa, 2)
                    weights_a(na, 7)
                if Bt:
                    weights_b(nb, pb, H1)
                if A:
                    outputs0(na, pa, 3)
                    dve.wait_ge(s_x1.sem, s_x1.after(na, H0 // 2))
                    statistics("b", na, X1[pa])
                    mean_shift("b", na)
                if Bt:
                    final(nb)

            joints(dve, joint)

        @block.tensor
        def _(pe):
            def claim(bk, n, k):
                if started(n, k):
                    pe.wait_ge(bk.free.sem, bk.free.after(n, k))

            def transpose_h(t, n, banks):
                pe.wait_ge(s_h[t].sem, s_h[t].after(n, NB))
                for k, bk in enumerate(banks):
                    claim(bk, n, 0)
                    for b in range(NB):
                        ins = pe.transpose(bk.t[:, b * P:(b + 1) * P], Hn[t][:, b, k * P:(k + 1) * P], ident[:])
                    ins.then_inc(bk.full.sem, 1)

            def score_rows(t, n, src, nk, bk, use):
                claim(bk, n, use)
                for k in range(nk):
                    ins = pe.matmul(bk.t[0:LO + heads[t], :], rows_w[t][:, k, :], src[:, k, :],
                                    start=(k == 0), stop=(k == nk - 1))
                ins.then_inc(bk.full.sem, 1)

            def h_ready(n, banks):
                for bk in banks:
                    pe.wait_ge(bk.free.sem, bk.free.after(n, 1))

            def transpose_scalars(t, n, rows_bank, rows_use, bk, use):
                pe.wait_ge(rows_bank.free.sem, rows_bank.free.after(n, rows_use))
                claim(bk, n, use)
                for b in range(NB):
                    ins = pe.transpose(bk.t[:, b * P:(b + 1) * P], RT[t][:, b * P:(b + 1) * P], ident[:])
                ins.then_inc(bk.full.sem, 1)

            def project0(n, half):
                bk = a_o[half]
                claim(bk, n, 1)
                for j in range(2):
                    b = 2 * half + j
                    for k in range(KB):
                        ins = pe.matmul(bk.t[:, j * D:(j + 1) * D], HT["a"][:, k, b * P:(b + 1) * P], WP[:, k, :],
                                        start=(k == 0), stop=(k == KB - 1))
                ins.then_inc(bk.full.sem, 1)

            def project1(n, b):
                bk = b_o[b % 2]
                claim(bk, n, 1 + b // 2)
                for k in range(KB):
                    ins = pe.matmul(bk.t[:], HT["b"][:, k, b * P:(b + 1) * P], W1[:, k, :],
                                    start=(k == 0), stop=(k == KB - 1))
                ins.then_inc(bk.full.sem, 1)

            def project2(n, half):
                bk = b_o[half]
                claim(bk, n, 7 + half)
                for j in range(2):
                    b = 2 * half + j
                    for k in range(FB):
                        ins = pe.matmul(bk.t[:, j * F2:(j + 1) * F2], GT[:, k, b * P:(b + 1) * P], W2[:, k, :],
                                        start=(k == 0), stop=(k == FB - 1))
                ins.then_inc(bk.full.sem, 1)

            def transpose_mask(n, p):
                pe.wait_ge(s_mask.sem, s_mask.after(n, 1))
                for half, (bk, use) in enumerate(((a_m, 1), (a_g, 0))):
                    claim(bk, n, use)
                    dst = bk.t[:].bitcast(BF16)
                    for jb in range(2):
                        j = 2 * half + jb
                        for b in range(NB):
                            ins = pe.transpose(dst[:, jb * N + b * P:jb * N + (b + 1) * P],
                                               MASK[p][:, b, j * P:(j + 1) * P], identb[:])
                    ins.then_inc(bk.full.sem, 1)

            def mean_row(n):
                claim(a_m, n, 3)
                for k in range(KB):
                    ins = pe.matmul(a_m.t[:, 0:D], hsum[:, k:k + 1].to_broadcast([P, P]), WP[:, k, :],
                                    start=(k == 0), stop=(k == KB - 1))
                ins.then_inc(a_m.full.sem, 1)

            def spread(t, n, h, bk, use):
                w = LO + heads[t]
                claim(bk, n, use)
                pe.wait_ge(s_gl[t].sem, s_gl[t].after(n, 1))
                pe.matmul(bk.t[:], pick[0:w, h, :], GS[t][:], start=True, stop=True).then_inc(bk.full.sem, 1)

            def spread_a(n, h):
                spread("a", n, h, a_g, 1 + h)

            def spread_b(n, h):
                if h < H1:
                    spread("b", n, h, b_g, h)
                else:
                    spread("c", n, 0, b_g, h)

            def sums0(n, h):
                bk = a_o[(h // 2) % 2]
                pe.wait_ge(s_w["a"].sem, s_w["a"].after(n, h + 1))
                if h == 0:
                    pe.wait_ge(s_den["a"].sem, s_den["a"].after(n, 1))
                    for o in a_o:
                        pe.wait_ge(o.free.sem, o.free.after(n, 2))
                if h % 2 == 0:
                    claim(bk, n, 2 + h // 4)
                for b in range(NB):
                    at = (2 * b + h % 2) * (K0 + 1)
                    for j in range(NB):
                        ins = pe.matmul(bk.t[:, at:at + K0 + 1], W["a"][h % 2][:, j, b * P:(b + 1) * P],
                                        V0[:, j, h, :], start=(j == 0), stop=(j == NB - 1))
                ins.then_inc(s_pv["a"].sem, 1)

            def sums1(n, p, h):
                pe.wait_ge(s_w["b"].sem, s_w["b"].after(n, h + 1))
                if h == 0:
                    pe.wait_ge(s_den["b"].sem, s_den["b"].after(n, 1))
                    for o in b_o:
                        pe.wait_ge(o.free.sem, o.free.after(n, 3))
                for b in range(NB):
                    bk = b_o[b // 2]
                    if b % 2 == 0:
                        claim(bk, n, 3 + h)
                    at = (b % 2) * (F1 + 1)
                    for j in range(NB):
                        ins = pe.matmul(bk.t[:, at:at + F1 + 1], W["b"][(p + h) % 2][:, j, b * P:(b + 1) * P],
                                        V1[:, j, h, :], start=(j == 0), stop=(j == NB - 1))
                    if b == 1:
                        ins.then_inc(s_half.sem, 1)
                ins.then_inc(s_pv["b"].sem, 1)

            def sums2(n, p):
                pe.wait_ge(s_w["b"].sem, s_w["b"].after(n, H1 + 1))
                for o, used in zip(b_o, (8, 9)):
                    pe.wait_ge(o.free.sem, o.free.after(n, used))
                for b in range(NB):
                    bk = b_o[b % 2]
                    if b >= 2:
                        pe.wait_ge(s_fin.sem, s_fin.after(n, b - 1))
                    for j in range(NB):
                        ins = pe.matmul(bk.t[:, 0:F2 + 1], W["b"][(p + H1) % 2][:, j, b * P:(b + 1) * P], V2[:, j, :],
                                        start=(j == 0), stop=(j == NB - 1))
                    if b < NB - 1:
                        ins.then_inc(s_half.sem, 1)
                ins.then_inc(s_pv["b"].sem, 1)

            def transpose_y(n, h):
                for o in b_o:
                    pe.wait_ge(o.free.sem, o.free.after(n, 4 + h))
                claim(b_m, n, 2 + h)
                for b in range(NB):
                    ins = pe.transpose(b_m.t[:, b * P:(b + 1) * P], Y[:, b, :], ident[:])
                ins.then_inc(b_m.full.sem, 1)

            def joint(nb, pb, na, pa):
                A, Bt = na is not None, nb is not None
                if Bt:
                    if started(nb):
                        pe.wait_ge(s_fin.sem, s_fin.after(nb - 1, NB))
                    transpose_h("b", nb, (b_m, b_o[0]))
                if A:
                    transpose_h("a", na, (a_m, a_o[0]))
                if Bt:
                    h_ready(nb, (b_m, b_o[0]))
                    score_rows("b", nb, HT["b"], KB, b_o[1], 0)
                if A:
                    h_ready(na, (a_m, a_o[0]))
                    score_rows("a", na, HT["a"], KB, a_o[1], 0)
                if Bt:
                    project1(nb, 0)
                if A:
                    project0(na, 0)
                    transpose_mask(na, pa)
                if Bt:
                    transpose_scalars("b", nb, b_o[1], 1, b_m, 1)
                if A:
                    transpose_scalars("a", na, a_o[1], 1, a_m, 2)
                    mean_row(na)
                    project0(na, 1)
                if Bt:
                    for b in range(1, NB):
                        project1(nb, b)
                    spread_b(nb, 0)
                if A:
                    spread_a(na, 0)
                for h in range(H1):
                    if Bt:
                        if h + 1 < H1:
                            spread_b(nb, h + 1)
                        sums1(nb, pb, h)
                        if h:
                            transpose_y(nb, h - 1)
                    if A:
                        spread_a(na, h + 1)
                        sums0(na, h)
                if A:
                    spread_a(na, 5)
                    sums0(na, 4)
                if Bt:
                    transpose_y(nb, H1 - 1)
                if A:
                    spread_a(na, 6)
                    sums0(na, 5)
                if Bt:
                    pe.wait_ge(s_gt.sem, s_gt.after(nb, H1))
                    score_rows("c", nb, GT, FB, b_o[1], 7)
                    project2(nb, 0)
                if A:
                    spread_a(na, 7)
                    sums0(na, 6)
                if Bt:
                    transpose_scalars("c", nb, b_o[1], 8, b_m, 6)
                    project2(nb, 1)
                    spread_b(nb, H1)
                if A:
                    sums0(na, 7)
                if Bt:
                    sums2(nb, pb)

            pe.wait_ge(cst.sem, 12)
            pe.wait_ge(w_in.sem, N_W)
            pe.wait_ge(cst_b.sem, 2)
            joints(pe, joint)


_INS = ['x', 'adj', 'L0_gnn_W_proj', 'L0_gnn_W_att', 'L0_gnn_b_att', 'L1_gnn_W1', 'L1_gnn_att_src1',
        'L1_gnn_att_dst1', 'L1_gnn_b1', 'L1_gnn_W2', 'L1_gnn_att_src2', 'L1_gnn_att_dst2', 'L1_gnn_b2']
_OUTS = [((16, 512, 256), 'float32')]


def kernel(**inputs):
    import numpy as _np
    import concourse.bacc as _bacc
    from concourse import mybir as _mybir
    from concourse.bass_utils import run_bass_kernel_spmd as _run

    nc = _bacc.Bacc("TRN2", target_bir_lowering=False, num_devices=1)
    arrays, args = {}, []
    for name in _INS:
        a = _np.ascontiguousarray(inputs[name])
        arrays[f"in_{name}_dram"] = a
        args.append(nc.dram_tensor(f"in_{name}_dram", a.shape, _mybir.dt.from_np(a.dtype), kind="ExternalInput").ap())
    for i, (shape, dtype) in enumerate(_OUTS):
        dt = _mybir.dt.from_np(_np.dtype(dtype))
        args.append(nc.dram_tensor(f"out_{i}_dram", shape, dt, kind="ExternalOutput").ap())
    gnn_kernel(nc, *args)
    r = _run(nc, [arrays], core_ids=[0])
    got = tuple(r.results[0][f"out_{i}_dram"] for i in range(len(_OUTS)))
    return got[0]
```

```python
from contextlib import ExitStack

import concourse.bass as bass
from concourse import mybir

ALU = mybir.AluOpType
ACT = mybir.ActivationFunctionType
AX_X = mybir.AxisListType.X
F32 = mybir.dt.float32
F32R = mybir.dt.float32r
BF16 = mybir.dt.bfloat16
I32 = mybir.dt.int32

P = 128
LO = 32
SLOPE = 0.2
EPS = 1e-5
LIFT = 60.0
TINY = 1e-37


class Signal:

    def __init__(self, sem, per_batch):
        self.sem, self.per_batch = sem, per_batch

    def after(self, n, k):
        return self.per_batch * n + k


class Bank:

    def __init__(self, tensor, full, free):
        self.t, self.full, self.free = tensor, full, free


def started(n, k=0):
    return not (isinstance(n, int) and n == 0 and k == 0)


def gnn_kernel(nc, x, adj, w_proj, w_att, b_att, w1, att_src1, att_dst1, b1, w2, att_src2, att_dst2, b2, out):
    B, N, D = x.shape
    H0, K2 = w_att.shape
    K0 = K2 // 2
    H1, F1 = att_src1.shape
    F2 = att_src2.shape[1]
    NB = N // P
    KB = D // P
    FB = H1 * F1 // P
    assert F1 == P and H0 * K0 == D and F2 == D and H0 % 4 == 0 and N == 512 and B % 2 == 0

    with ExitStack() as ctx:
        def sb(name, shape, dt=F32):
            return ctx.enter_context(nc.sbuf_tensor(name, shape, dt))

        def signal(name, per_batch=1):
            return Signal(ctx.enter_context(nc.semaphore(name)), per_batch)

        def bank(name, full, free):
            return Bank(ctx.enter_context(nc.psum_tensor(name, [P, 512], F32)),
                        signal(name + "_full", full), signal(name + "_free", free))

        a_m = bank("a_m", 6, 6)
        a_o = [bank("a_o0", 3, 7), bank("a_o1", 3, 7)]
        a_g = bank("a_g", 1 + H0, 1 + H0)
        b_m = bank("b_m", 4 + H1, 4 + H1)
        b_g = bank("b_g", H1 + 2, H1 + 2)
        b_o = [bank("b_o0", 3, 7), bank("b_o1", 4, 8)]

        WP = sb("WP", [P, KB, D])
        W1 = sb("W1", [P, KB, H1 * F1])
        W2 = sb("W2", [P, FB, F2])
        C0 = K0 + 1
        rest_store = sb("rest_store", [P, NB * H0 * 2 * C0])
        REST = rest_store[:].rearrange("p (b h u c) -> p b h u c", b=NB, h=H0, u=2)
        XN = rest_store[:, 0:NB * D].rearrange("p (b d) -> p b d", b=NB)
        XM = rest_store[:, NB * D:2 * NB * D].rearrange("p (b d) -> p b d", b=NB)
        v0_store = sb("v0_store", [P, NB * H0 * 2 * C0])
        pick32 = v0_store[0:LO + H0, 512:512 + H0 * P].rearrange("k (h m) -> k h m", h=H0)
        V0 = v0_store[:].rearrange("p (b h u c) -> p b h u c", b=NB, h=H0, u=2)
        SUMS = v0_store[:, 0:H0 * NB * C0].rearrange("p (h b c) -> p h b c", h=H0, b=NB)
        T = v0_store[:, H0 * NB * C0:H0 * NB * (C0 + K0)].rearrange("p (h b c) -> p h b c", h=H0, b=NB)
        rows_w = {"a": sb("rows_w0", [P, KB, LO + H0]), "b": sb("rows_w1", [P, KB, LO + H1]),
                  "c": sb("rows_w2", [P, FB, LO + 1])}
        batt = sb("batt", [H0, 1])
        b1c = sb("b1c", [P, H1])
        b2r = sb("b2r", [P, F2])
        ident = sb("ident", [P, P])
        identb = sb("identb", [P, P], BF16)
        pick = sb("pick", [LO + H0, H0, P], F32R)
        lift = sb("lift", [P, 1])
        one = sb("one", [P, 1])
        b1n = sb("b1n", [P, H1])
        power = sb("power", [P, NB])
        warm = sb("warm", [P, 1])

        X = [sb(f"X{p}", [P, NB, D]) for p in range(2)]
        ADJ = sb("ADJ", [P, NB, N], I32)
        MASK = [sb(f"MASK{p}", [P, NB, N], BF16) for p in range(2)]
        MASKT = sb("MASKT", [P, NB, N], BF16)
        NOEDGE = sb("NOEDGE", [P, NB, N], BF16)
        X1 = [sb(f"X1{p}", [P, NB, D]) for p in range(2)]
        OUT = sb("OUT", [P, NB, F2])
        RM = sb("RM", [P, D])
        hsum = sb("hsum", [P, KB])
        none = sb("none", [P, NB])
        stats = {t: sb("stats_" + t, [P, NB, 6]) for t in "ab"}
        mv = {t: sb("mv_" + t, [P, NB, 5]) for t in "ab"}
        veps = {t: sb("veps_" + t, [P, NB]) for t in "ab"}
        rstd = {t: sb("rstd_" + t, [P, NB]) for t in "ab"}
        shift = {t: sb("shift_" + t, [P, NB]) for t in "ab"}
        Hn = {"a": XN, "b": sb("H_b", [P, NB, D])}
        GT = sb("GT", [P, FB, N])
        HT = {"a": sb("HT_a", [P, KB, N]), "b": GT[:, 0:KB]}
        heads = {"a": H0, "b": H1, "c": 1}
        top = {t: sb("top_" + t, [LO + H0, 1]) for t in "abc"}
        atop = {t: sb("atop_" + t, [H0, 1]) for t in "abc"}
        top8 = {t: sb("top8_" + t, [LO + H0, 1]) for t in "abc"}
        top2 = {t: sb("top2_" + t, [LO + H0, 1]) for t in "abc"}
        top2lo = {t: sb("top2lo_" + t, [H0, 1]) for t in "abc"}
        Z = {"a": sb("Z_a", [H0, N]), "b": sb("Z_b", [H1, N])}
        GS = {"a": sb("GS_a", [LO + H0, N], F32R), "b": sb("GS_b", [LO + H1, N], F32R)}
        RT = {"a": sb("RT_a", [P, N]), "b": sb("RT_b", [P, N])}
        for rows in (Z, GS, RT):
            rows["c"] = rows["b"]
        SC = {t: sb("SC_" + t, [P, NB, (2 * LO if t == "a" else LO) + heads[t]]) for t in "abc"}
        PARTS = sb("PARTS", [P, 3, NB, H0, 2, C0], BF16)
        SIGN = [sb(f"SIGN{q}", [P, NB, N], BF16) for q in range(2)]
        HIGH = [sb(f"HIGH{q}", [P, NB, N], BF16) for q in range(2)]
        MS = sb("MS", [P, NB, H0, C0])
        SS = [sb(f"SS{q}", [P, NB, 2, C0]) for q in range(2)]
        LOWS = sb("LOWS", [P, NB, C0])
        GLOWS = sb("GLOWS", [P, NB, C0])
        V1 = sb("V1", [P, NB, H1, F1 + 1])
        V2 = V1[:].rearrange("p b h c -> p (b h c)")[:, 0:NB * (F2 + 1)].rearrange("p (b c) -> p b c", b=NB)
        GB = [sb(f"GB{q}", [P, N]) for q in range(2)]
        W = [sb(f"weights{q}", [P, NB, N]) for q in range(2)]
        att_store, prod = (w[:].rearrange("p b i -> p (b i)") for w in W)
        att0 = att_store[:, 0:H0 * K2].rearrange("p (h c) -> p h c", h=H0)
        att1 = att_store[:, 512:1536].rearrange("p (s h c) -> p s h c", s=2, h=H1)
        att2 = att_store[:, 1536:2048].rearrange("p (s c) -> p s c", s=2)
        den = {t: sb("den_" + t, [P, 16]) for t in "ab"}
        rden = {t: sb("rden_" + t, [P, 16]) for t in "ab"}
        Y = sb("Y", [P, NB, F1])
        EX = sb("EX", [P, N])
        RL = sb("RL", [P, N])

        wa_in = signal("weights_in_a", 16 * 3)
        wb_in = signal("weights_in_b", 16 * 8)
        folded = {t: signal("folded_" + t, 2) for t in "abc"}
        cst = signal("cst")
        cst_b = signal("cst_b")
        setup = signal("setup")
        x_in = [signal(f"x_in{p}", 8) for p in range(2)]
        adj_in = signal("adj_in", 16)
        s_bn = {t: signal("bn_" + t, NB) for t in "ab"}
        s_mv = {t: signal("mv_done_" + t, 5) for t in "ab"}
        s_ve = {t: signal("veps_done_" + t) for t in "ab"}
        s_rstd = {t: signal("rstd_done_" + t) for t in "ab"}
        s_shift = {t: signal("shift_done_" + t) for t in "ab"}
        s_h = {t: signal("h_done_" + t, NB) for t in "ab"}
        s_top = {t: signal("top_done_" + t) for t in "abc"}
        s_small = {t: signal("small_done_" + t, 4) for t in "abc"}
        s_z = {t: signal("z_done_" + t) for t in "abc"}
        s_g = {t: signal("g_done_" + t) for t in "abc"}
        s_ga = signal("gates_to_transpose")
        s_gh = {t: signal("g_high_" + t) for t in "abc"}
        s_gl = {t: signal("g_low_" + t) for t in "abc"}
        s_den = {t: signal("den_col_" + t) for t in "abc"}
        s_mask = signal("mask_done")
        s_diag = signal("diag_done", 2)
        s_noedge = signal("noedge_done")
        s_w = {"a": signal("weights_a", H0), "b": signal("weights_b", H1 + 1)}
        s_pv = {"a": signal("sums_a", H0), "b": signal("sums_b", H1 + 1)}
        s_half = signal("half_sums_b", H1 + NB - 1)
        s_den_r = {"a": signal("den_a", 2), "b": signal("den_b", 2 * H1 + NB)}
        s_rden = {"a": signal("rden_a", 2), "b": signal("rden_b", 2 * H1 + NB)}
        s_none = signal("none_done")
        s_xn = signal("xn_done")
        s_xm = signal("xm_done")
        s_v0 = signal("v0_done", 2)
        s_u = signal("u_done", 2)
        s_hi = signal("high_part", 2)
        s_rest = signal("rest_done", 2)
        s_mid = signal("middle_part", 2)
        s_lo = signal("low_part", 2)
        s_lows = signal("lows_done", H0)
        s_glows = signal("glows_done", H0)
        s_sums = signal("sums_done", H0)
        s_t = signal("outputs_a", 2)
        s_x1 = signal("x1_done", 2)
        s_ex = signal("exp_done", H1)
        s_em = signal("em_done", H1 - 1)
        s_gt = signal("gt_done", H1)
        s_x1b = signal("x1b_done")
        s_fin = signal("fin_done", NB)
        s_out = signal("out_done", 16)

        block = ctx.enter_context(nc.Block())

        @block.sync
        def _(sp):
            def load(n, p):
                if started(n) and not (isinstance(n, int) and n < 2):
                    sp.wait_ge(s_xm.sem, s_xm.after(n - 2, 1))
                sp.dma_start(X[p][:], x[n].rearrange("(b p) d -> p b d", p=P)).then_inc(x_in[p].sem, 16)
                if started(n):
                    sp.wait_ge(s_mask.sem, s_mask.after(n - 1, 1))
                sp.dma_start(ADJ[:], adj[n].rearrange("(b p) j -> p b j", p=P)).then_inc(adj_in.sem, 16)

            def store(n):
                sp.wait_ge(s_fin.sem, s_fin.after(n, NB))
                sp.dma_start(out[n].rearrange("(b p) d -> p b d", p=P), OUT[:]).then_inc(s_out.sem, 16)

            load(0, 0)
            for dst, src, done in (
                (WP[:], w_proj.rearrange("(k p) o -> p k o", p=P), wa_in),
                (att0, w_att.partition_broadcast(P), wa_in),
                (batt[:], b_att.rearrange("(h a) -> h a", a=1), wa_in),
                (W1[:], w1.rearrange("(k p) o -> p k o", p=P), wb_in),
                (W2[:], w2.rearrange("(k p) o -> p k o", p=P), wb_in),
                (att1[:, 0], att_dst1.partition_broadcast(P), wb_in),
                (att1[:, 1], att_src1.partition_broadcast(P), wb_in),
                (att2[:, 0], att_dst2[0].partition_broadcast(P), wb_in),
                (att2[:, 1], att_src2[0].partition_broadcast(P), wb_in),
                (b2r[:], b2.partition_broadcast(P), wb_in),
                (b1c[:], b1.rearrange("(h p) -> p h", p=P), wb_in),
            ):
                with nc.allow_non_contiguous_dma(reason="two short vectors, once"):
                    sp.dma_start(dst, src).then_inc(done.sem, 16)
            load(1, 1)
            with sp.Fori(0, B // 2 - 1) as i:
                for p in range(2):
                    load(2 * i + 2 + p, p)
                    store(2 * i + p)
            store(B - 2)
            store(B - 1)
            sp.wait_ge(s_out.sem, s_out.after(B - 1, 16))

        def joints(engine, joint):
            joint(None, None, None, None, 0, 0)
            joint(None, None, 0, 0, 1, 1)
            joint(0, 0, 1, 1, 2, 0)
            with engine.Fori(0, B // 2 - 2) as i:
                joint(2 * i + 1, 1, 2 * i + 2, 0, 2 * i + 3, 1)
                joint(2 * i + 2, 0, 2 * i + 3, 1, 2 * i + 4, 0)
            joint(B - 3, 1, B - 2, 0, B - 1, 1)
            joint(B - 2, 0, B - 1, 1, None, None)
            joint(B - 1, 1, None, None, None, None)

        @block.gpsimd
        def _(pool):
            pool.memset(ident[:], 0.0).then_inc(cst.sem, 1)
            pool.memset(pick32, 0.0).then_inc(cst.sem, 1)
            pool.memset(lift[:], LIFT).then_inc(cst.sem, 1)
            pool.memset(power[:], -0.5).then_inc(cst.sem, 1)
            pool.memset(one[:], 1.0).then_inc(cst.sem, 1)
            pool.wait_ge(cst.sem, 5)
            pool.affine_select(out=ident[:], in_=ident[:], compare_op=ALU.not_equal, fill=1.0, base=0,
                               pattern=[[-1, P]], channel_multiplier=1).then_inc(cst.sem, 1)
            pool.affine_select(out=pick32, in_=pick32, compare_op=ALU.not_equal, fill=1.0, base=0,
                               pattern=[[-1, H0], [0, P]], channel_multiplier=1).then_inc(cst.sem, 1)
            pool.wait_ge(cst.sem, 7)
            pool.affine_select(out=pick32, in_=pick32, compare_op=ALU.not_equal, fill=1.0, base=-LO,
                               pattern=[[-1, H0], [0, P]], channel_multiplier=1).then_inc(cst.sem, 1)
            pool.tensor_copy(identb[:], ident[:]).then_inc(cst.sem, 1)
            for t in "ab":
                pool.memset(RT[t][:], 0.0).then_inc(cst.sem, 1)
            pool.wait_ge(cst.sem, 11)

            def rstd_of(t, n):
                pool.wait_ge(s_ve[t].sem, s_ve[t].after(n, 1))
                pool.tensor_tensor(rstd[t][:], veps[t][:], power[:], ALU.pow).then_inc(s_rstd[t].sem, 1)

            def elu(n, h):
                pool.wait_ge(s_ex.sem, s_ex.after(n, h + 1))
                pool.tensor_tensor(EX[:], EX[:], one[:].to_broadcast([P, N]), ALU.subtract).then_inc(s_em.sem, 1)
                pool.wait_ge(s_em.sem, s_em.after(n, h + 1))
                pool.tensor_tensor(GT[:, h, :], EX[:], RL[:], ALU.add).then_inc(s_gt.sem, 1)

            def low_part(n, half):
                pool.wait_ge(s_mid.sem, s_mid.after(n, half + 1))
                b = slice(2 * half, 2 * half + 2)
                pool.tensor_tensor(PARTS[:, 2, b], REST[:, b], PARTS[:, 1, b], ALU.subtract).then_inc(s_lo.sem, 1)

            def x_and_mean(n, p):
                pool.wait_ge(s_none.sem, s_none.after(n, 1))
                pool.tensor_tensor(XN, RM[:].unsqueeze(1).to_broadcast([P, NB, D]),
                                   none[:].unsqueeze(2).to_broadcast([P, NB, D]), ALU.mult).then_inc(s_xn.sem, 1)
                pool.wait_ge(s_xn.sem, s_xn.after(n, 1))
                pool.tensor_tensor(XM, XN, X[p][:], ALU.add).then_inc(s_xm.sem, 1)

            def combine(n, h):
                pool.wait_ge(a_o[h % 2].free.sem, a_o[h % 2].free.after(n, 4 + h // 2))
                pool.tensor_tensor(LOWS[:], MS[:, :, h], SS[h % 2][:, :, 1], ALU.subtract).then_inc(s_lows.sem, 1)
                pool.wait_ge(s_lows.sem, s_lows.after(n, h + 1))
                pool.tensor_tensor(GLOWS[:], LOWS[:], SC["a"][:, :, 2 * LO + h:2 * LO + h + 1].to_broadcast([P, NB, C0]),
                                   ALU.mult).then_inc(s_glows.sem, 1)
                pool.wait_ge(s_glows.sem, s_glows.after(n, h + 1))
                pool.tensor_tensor(SUMS[:, h], GLOWS[:], SS[h % 2][:, :, 0], ALU.add).then_inc(s_sums.sem, 1)

            def x1(n, p, half):
                pool.wait_ge(s_t.sem, s_t.after(n, half + 1))
                h = slice(4 * half, 4 * half + 4)
                pool.tensor_tensor(X1[p][:].rearrange("p b (h c) -> p h b c", c=K0)[:, h], T[:, h],
                                   XM.rearrange("p b (h c) -> p h b c", c=K0)[:, h], ALU.add).then_inc(s_x1.sem, 1)

            def x1b(n, p):
                if started(n):
                    pool.wait_ge(s_out.sem, s_out.after(n - 1, 16))
                pool.tensor_tensor(OUT[:], X1[p][:], b2r[:].unsqueeze(1).to_broadcast([P, NB, F2]),
                                   ALU.add).then_inc(s_x1b.sem, 1)

            def joint(nb, pb, na, pa, nx, px):
                A, Bt, NX = na is not None, nb is not None, nx is not None
                if Bt:
                    if not started(nb):
                        pool.wait_ge(wb_in.sem, wb_in.after(0, 16 * 8))
                    x1b(nb, pb)
                if A:
                    x_and_mean(na, pa)
                    combine(na, 0)
                for h in range(H1):
                    if Bt and h >= 1:
                        elu(nb, h - 1)
                    if NX and h == 0:
                        rstd_of("a", nx)
                    if A:
                        combine(na, h + 1)
                if A:
                    x1(na, pa, 0)
                    combine(na, 5)
                    combine(na, 6)
                    combine(na, 7)
                    x1(na, pa, 1)
                    rstd_of("b", na)
                if NX:
                    low_part(nx, 0)

            joints(pool, joint)

        @block.scalar
        def _(act):
            act.wait_ge(cst.sem, 11)
            act.activation(warm[:], one[:], ACT.Exp)

            def normalize(t, n, src):
                act.wait_ge(s_shift[t].sem, s_shift[t].after(n, 1))
                if t == "a" and started(n):
                    act.wait_ge(s_xm.sem, s_xm.after(n - 1, 1))
                for b in range(NB):
                    act.activation(Hn[t][:, b, :], src[:, b, :], ACT.Relu, bias=shift[t][:, b:b + 1],
                                   scale=rstd[t][:, b:b + 1]).then_inc(s_h[t].sem, 1)

            def h_transposed(t, n, k, bk, use):
                act.wait_ge(bk.full.sem, bk.full.after(n, use))
                act.activation(HT[t][:, k, :], bk.t[:], ACT.Copy,
                               accum_out=hsum[:, k:k + 1] if t == "a" else None).then_inc(bk.free.sem, 1)

            def row_exps(t, n, bk, use):
                nh = heads[t]
                act.wait_ge(s_small[t].sem, s_small[t].after(n, 4))
                act.activation(RT[t][LO:LO + nh, :], bk.t[LO:LO + nh, :], ACT.Exp, bias=top8[t][LO:LO + nh, :],
                               scale=1.0 - SLOPE)
                act.wait_ge(s_z[t].sem, s_z[t].after(n, 1))
                act.activation(RT[t][0:nh, :], bk.t[LO:LO + nh, :], ACT.Exp, bias=top2[t][LO:LO + nh, :],
                               scale=SLOPE).then_inc(bk.free.sem, 1)
                if t == "a":
                    act.activation(RT[t][2 * LO:2 * LO + nh, :], Z[t][0:nh, :], ACT.Exp, bias=lift[0:nh, :],
                                   scale=SLOPE - 1.0).then_inc(s_ga.sem, 1)
                act.activation(Z[t][0:nh, :], Z[t][0:nh, :], ACT.Exp, bias=lift[0:nh, :],
                               scale=SLOPE - 1.0).then_inc(s_g[t].sem, 1)
                act.wait_ge(s_g[t].sem, s_g[t].after(n, 1))
                act.activation(GS[t][0:nh, :], Z[t][0:nh, :], ACT.Copy).then_inc(s_gh[t].sem, 1)

            def mask_transposed(n):
                for half, (bk, use) in enumerate(((a_m, 5), (a_g, 1))):
                    act.wait_ge(bk.full.sem, bk.full.after(n, use))
                    act.activation(MASKT[:, 2 * half:2 * half + 2, :],
                                   bk.t[:].bitcast(BF16).rearrange("p (b i) -> p b i", b=2),
                                   ACT.Copy).then_inc(bk.free.sem, 1)

            def high_parts(n, half):
                act.wait_ge(s_u.sem, s_u.after(n, half + 1))
                b = slice(2 * half, 2 * half + 2)
                act.activation(PARTS[:, 0, b], V0[:, b], ACT.Copy).then_inc(s_hi.sem, 1)

            def middle_parts(n, half):
                act.wait_ge(s_rest.sem, s_rest.after(n, half + 1))
                b = slice(2 * half, 2 * half + 2)
                act.activation(PARTS[:, 1, b], REST[:, b], ACT.Copy).then_inc(s_mid.sem, 1)

            def all_lows(n, blocks):
                if started(n) and blocks[0] == 0:
                    act.wait_ge(s_sums.sem, s_sums.after(n - 1, H0))
                for b in blocks:
                    bk = a_o[b % 2]
                    act.wait_ge(bk.full.sem, bk.full.after(n, 2 + b // 2))
                    act.activation(MS[:, b], bk.t[:, 0:H0 * C0].rearrange("p (h c) -> p h c", c=C0),
                                   ACT.Copy).then_inc(bk.free.sem, 1)

            def signs(n, h):
                act.wait_ge(a_g.full.sem, a_g.full.after(n, h + 2))
                if h == 0:
                    act.wait_ge(a_m.free.sem, a_m.free.after(n, 4))
                if not (isinstance(n, int) and n == 0 and h < 2):
                    act.wait_ge(s_w["a"].sem, s_w["a"].after(n, h - 1))
                for b in range(NB):
                    ins = act.activation(SIGN[h % 2][:, b, :], a_g.t[:], ACT.Sign, scale=-1.0,
                                         bias=SC["a"][:, b, LO + h:LO + h + 1])
                ins.then_inc(a_g.free.sem, 1)

            def head_sums(n, h):
                bk = a_o[h % 2]
                act.wait_ge(s_pv["a"].sem, s_pv["a"].after(n, h + 1))
                if not (isinstance(n, int) and n == 0 and h < 2):
                    act.wait_ge(s_sums.sem, s_sums.after(n, h - 1))
                act.activation(SS[h % 2][:], bk.t[:, 0:NB * 2 * C0].rearrange("p (b u c) -> p b u c", b=NB, u=2),
                               ACT.Copy).then_inc(bk.free.sem, 1)

            def mean_row(n):
                act.wait_ge(a_m.full.sem, a_m.full.after(n, 6))
                act.activation(RM[:], a_m.t[:, 0:D], ACT.Relu, scale=1.0 / N).then_inc(a_m.free.sem, 1)

            def gates_b(n, p, h):
                q = (p + h) % 2
                act.wait_ge(b_g.full.sem, b_g.full.after(n, h + 2))
                if not (isinstance(n, int) and n == 0 and h < 2):
                    act.wait_ge(s_w["b"].sem, s_w["b"].after(n, h - 1))
                act.activation(GB[q][:], b_g.t[:], ACT.Copy).then_inc(b_g.free.sem, 1)

            def elu_parts(n, h):
                act.wait_ge(b_m.full.sem, b_m.full.after(n, 4 + h))
                if started(n, h):
                    act.wait_ge(s_gt.sem, s_gt.after(n, h))
                act.activation(RL[:], b_m.t[:], ACT.Relu, bias=b1c[:, h:h + 1])
                act.activation(EX[:], b_m.t[:], ACT.Relu, bias=b1n[:, h:h + 1], scale=-1.0).then_inc(b_m.free.sem, 1)
                act.wait_ge(b_m.free.sem, b_m.free.after(n, 4 + h))
                act.activation(EX[:], EX[:], ACT.Exp, scale=-1.0).then_inc(s_ex.sem, 1)

            def values2(n, half):
                bk = b_o[half]
                act.wait_ge(s_den["c"].sem, s_den["c"].after(n, 1))
                act.wait_ge(bk.full.sem, bk.full.after(n, 3 + half))
                for j in range(2):
                    b = 2 * half + j
                    ins = act.activation(V2[:, b, 0:F2], bk.t[:, j * F2:(j + 1) * F2], ACT.Copy,
                                         scale=SC["c"][:, b, 0:1])
                ins.then_inc(bk.free.sem, 1)

            def joint(nb, pb, na, pa, nx, px):
                A, Bt, NX = na is not None, nb is not None, nx is not None
                if A:
                    signs(na, 0)
                if Bt:
                    if not started(nb):
                        act.wait_ge(wb_in.sem, wb_in.after(0, 16 * 8))
                        act.wait_ge(cst_b.sem, 2)
                    row_exps("b", nb, b_m, 2)
                if A:
                    all_lows(na, (0, 1))
                    signs(na, 1)
                    all_lows(na, (2, 3))
                if Bt:
                    gates_b(nb, pb, 0)
                if A:
                    signs(na, 2)
                    head_sums(na, 0)
                for h in range(H1):
                    if Bt and h + 1 < H1:
                        gates_b(nb, pb, h + 1)
                    if Bt and h >= 1:
                        elu_parts(nb, h - 1)
                    if A:
                        head_sums(na, h + 1)
                        signs(na, h + 3)
                    if NX and h == 2:
                        act.wait_ge(x_in[px].sem, x_in[px].after(nx, 16 - 8 * px))
                        normalize("a", nx, X[px])
                if NX:
                    h_transposed("a", nx, 0, a_m, 1)
                if Bt:
                    elu_parts(nb, 3)
                if NX:
                    h_transposed("a", nx, 1, a_m, 2)
                if A:
                    head_sums(na, 5)
                    signs(na, 7)
                    head_sums(na, 6)
                if NX:
                    row_exps("a", nx, a_m, 3)
                if Bt:
                    row_exps("c", nb, b_o[1], 7)
                if A:
                    head_sums(na, 7)
                if Bt:
                    gates_b(nb, pb, H1)
                    values2(nb, 0)
                    values2(nb, 1)
                if A:
                    normalize("b", na, X1[pa])
                if NX:
                    high_parts(nx, 0)
                if A:
                    h_transposed("b", na, 0, b_m, 1)
                    h_transposed("b", na, 1, b_g, 1)
                if NX:
                    mask_transposed(nx)
                    high_parts(nx, 1)
                    middle_parts(nx, 0)
                    middle_parts(nx, 1)
                    mean_row(nx)

            joints(act, joint)

        @block.vector
        def _(dve):
            dve.memset(rows_w["a"][:], 0.0)
            dve.memset(rows_w["b"][:], 0.0)
            dve.memset(rows_w["c"][:], 0.0).then_inc(setup.sem, 1)
            for t in "ab":
                dve.memset(GS[t][:].bitcast(F32), 0.0).then_inc(setup.sem, 1)
            dve.wait_ge(cst.sem, 11)
            dve.tensor_copy(pick[:], pick32).then_inc(cst_b.sem, 1)
            dve.wait_ge(setup.sem, 3)

            def fold(t, s):
                w, att, nh = {"a": (WP, att0[:, :, s * K0:(s + 1) * K0], H0), "b": (W1, att1[:, s], H1),
                              "c": (W2, att2[:, s:s + 1], 1)}[t]
                w = w[:].rearrange("p k (h c) -> p k h c", h=nh)
                nk, c = w.shape[1], w.shape[3]
                pr = prod[:, s * 1024:s * 1024 + nk * nh * c].rearrange("p (k h c) -> p k h c", k=nk, h=nh)
                if t != "a" and s == 0:
                    before = folded["abc"["abc".index(t) - 1]]
                    dve.wait_ge(before.sem, before.after(0, 2))
                if t == "a" and s == 0:
                    dve.wait_ge(wa_in.sem, wa_in.after(0, 16 * 3))
                if t == "b" and s == 0:
                    dve.wait_ge(wb_in.sem, wb_in.after(0, 16 * 8))
                    dve.tensor_scalar(b1n[:], b1c[:], -1.0, None, ALU.mult).then_inc(cst_b.sem, 1)
                dve.tensor_tensor(pr, w, att.unsqueeze(1).to_broadcast([P, nk, nh, c]), ALU.mult).then_inc(setup.sem, 1)
                dve.wait_ge(setup.sem, 4 + 2 * "abc".index(t) + s)
                dve.tensor_reduce(rows_w[t][:, :, s * LO:s * LO + nh], pr, AX_X, ALU.add).then_inc(folded[t].sem, 1)

            def statistics(t, n, src):
                for b in range(NB):
                    dve.bn_stats(stats[t][:, b, :], src[:, b, :]).then_inc(s_bn[t].sem, 1)
                dve.wait_ge(s_bn[t].sem, s_bn[t].after(n, NB))
                even, odd = stats[t][:, :, 0:3], stats[t][:, :, 3:6]
                dve.tensor_tensor(mv[t][:, :, 0], even[:, :, 1], odd[:, :, 1], ALU.add).then_inc(s_mv[t].sem, 1)
                dve.tensor_tensor(mv[t][:, :, 1], even[:, :, 1], odd[:, :, 1], ALU.subtract).then_inc(s_mv[t].sem, 1)
                dve.tensor_tensor(mv[t][:, :, 2], even[:, :, 2], odd[:, :, 2], ALU.add).then_inc(s_mv[t].sem, 1)
                dve.wait_ge(s_mv[t].sem, s_mv[t].after(n, 3))
                dve.scalar_tensor_tensor(mv[t][:, :, 3], mv[t][:, :, 1], 0.25, mv[t][:, :, 1], ALU.mult,
                                         ALU.mult).then_inc(s_mv[t].sem, 1)
                dve.tensor_scalar(mv[t][:, :, 4], mv[t][:, :, 2], 1.0 / D, EPS, ALU.mult,
                                  ALU.add).then_inc(s_mv[t].sem, 1)
                dve.wait_ge(s_mv[t].sem, s_mv[t].after(n, 5))
                if started(n):
                    dve.wait_ge(s_h[t].sem, s_h[t].after(n - 1, NB))
                dve.tensor_tensor(veps[t][:], mv[t][:, :, 3], mv[t][:, :, 4], ALU.add).then_inc(s_ve[t].sem, 1)

            def mean_shift(t, n):
                dve.wait_ge(s_rstd[t].sem, s_rstd[t].after(n, 1))
                dve.scalar_tensor_tensor(shift[t][:], mv[t][:, :, 0], -0.5, rstd[t][:], ALU.mult,
                                         ALU.mult).then_inc(s_shift[t].sem, 1)

            def bounds(t, n, bk, use):
                nh = heads[t]
                dve.wait_ge(bk.full.sem, bk.full.after(n, use))
                dve.tensor_reduce(top[t][LO:LO + nh, :], bk.t[LO:LO + nh, :], AX_X, ALU.max).then_inc(s_top[t].sem, 1)
                dve.wait_ge(s_top[t].sem, s_top[t].after(n, 1))
                if t == "a":
                    dve.tensor_copy(top2lo[t][0:nh, :], top[t][LO:LO + nh, :]).then_inc(s_small[t].sem, 1)
                    dve.wait_ge(s_small[t].sem, s_small[t].after(n, 1))
                    dve.tensor_tensor(atop[t][0:nh, :], top2lo[t][0:nh, :], batt[:], ALU.add).then_inc(s_small[t].sem, 1)
                else:
                    dve.tensor_copy(atop[t][0:nh, :], top[t][LO:LO + nh, :]).then_inc(s_small[t].sem, 2)
                dve.tensor_scalar(top8[t][LO:LO + nh, :], top[t][LO:LO + nh, :], SLOPE - 1.0, LIFT, ALU.mult,
                                  ALU.add).then_inc(s_small[t].sem, 1)
                dve.tensor_scalar(top2[t][LO:LO + nh, :], top[t][LO:LO + nh, :], -SLOPE, None,
                                  ALU.mult).then_inc(s_small[t].sem, 1)
                dve.wait_ge(s_small[t].sem, s_small[t].after(n, 4))
                dve.tensor_scalar(Z[t][0:nh, :], bk.t[0:nh, :], atop[t][0:nh, :], 0.0, ALU.add,
                                  ALU.max).then_inc(s_z[t].sem, 1)

            def gate_low(t, n):
                nh = heads[t]
                dve.wait_ge(s_gh[t].sem, s_gh[t].after(n, 1))
                dve.tensor_tensor(GS[t][LO:LO + nh, :], Z[t][0:nh, :], GS[t][0:nh, :].bitcast(F32),
                                  ALU.subtract).then_inc(s_gl[t].sem, 1)

            def scalars(t, n, bk, use, dst):
                w = (2 * LO if t == "a" else LO) + heads[t]
                dve.wait_ge(bk.full.sem, bk.full.after(n, use))
                dve.tensor_copy(SC[t][:], bk.t[:].rearrange("p (b w) -> p b w", b=NB)[:, :, 0:w]).then_inc(bk.free.sem, 1)
                dve.wait_ge(bk.free.sem, bk.free.after(n, use))
                if dst is not None:
                    dve.tensor_copy(dst, SC[t][:, :, 0:heads[t]]).then_inc(s_den[t].sem, 1)

            def values0(n, half):
                bk = a_o[half]
                if half == 0:
                    dve.tensor_copy(V0[:, :, :, 1, K0], SC["a"][:, :, 0:H0]).then_inc(s_den["a"].sem, 1)
                dve.wait_ge(bk.full.sem, bk.full.after(n, 1))
                for j in range(2):
                    b = 2 * half + j
                    ins = dve.tensor_tensor(V0[:, b, :, 1, 0:K0],
                                            bk.t[:, j * D:(j + 1) * D].rearrange("p (h c) -> p h c", h=H0),
                                            SC["a"][:, b, 0:H0].unsqueeze(2).to_broadcast([P, H0, K0]), ALU.mult)
                ins.then_inc(bk.free.sem, 1)
                dve.wait_ge(bk.free.sem, bk.free.after(n, 1))
                dve.wait_ge(s_den["a"].sem, s_den["a"].after(n, 1))
                for j in range(2):
                    b = 2 * half + j
                    ins = dve.tensor_tensor(V0[:, b, :, 0, :], V0[:, b, :, 1, :],
                                            SC["a"][:, b, LO:LO + H0].unsqueeze(2).to_broadcast([P, H0, C0]), ALU.mult)
                ins.then_inc(s_u.sem, 1)

            def rests(n, half):
                dve.wait_ge(s_hi.sem, s_hi.after(n, half + 1))
                if started(n):
                    dve.wait_ge(s_lo.sem, s_lo.after(n - 1, 2))
                b = slice(2 * half, 2 * half + 2)
                dve.tensor_tensor(REST[:, b], V0[:, b], PARTS[:, 0, b], ALU.subtract).then_inc(s_rest.sem, 1)

            def low_part(n, half):
                dve.wait_ge(s_mid.sem, s_mid.after(n, half + 1))
                b = slice(2 * half, 2 * half + 2)
                dve.tensor_tensor(PARTS[:, 2, b], REST[:, b], PARTS[:, 1, b], ALU.subtract).then_inc(s_lo.sem, 1)

            def elu(n, h):
                dve.wait_ge(s_ex.sem, s_ex.after(n, h + 1))
                dve.scalar_tensor_tensor(GT[:, h, :], EX[:], -1.0, RL[:], ALU.add, ALU.add).then_inc(s_gt.sem, 1)

            def lonely(n):
                for bk in a_o:
                    dve.wait_ge(bk.free.sem, bk.free.after(n, 3))
                dve.tensor_scalar(none[:], MS[:, :, 0, K0], 0.0, None, ALU.is_equal).then_inc(s_none.sem, 1)

            def values1(n, b):
                bk = b_o[b % 2]
                dve.wait_ge(bk.full.sem, bk.full.after(n, 1 + b // 2))
                dve.tensor_tensor(V1[:, b, :, 0:F1], bk.t[:].rearrange("p (h c) -> p h c", h=H1),
                                  SC["b"][:, b, 0:H1].unsqueeze(2).to_broadcast([P, H1, F1]),
                                  ALU.mult).then_inc(bk.free.sem, 1)

            def weights_a(n, h):
                if h == 0:
                    dve.wait_ge(s_noedge.sem, s_noedge.after(n, 1))
                dve.wait_ge(a_g.free.sem, a_g.free.after(n, h + 2))
                if not (isinstance(n, int) and n == 0 and h < 2):
                    dve.wait_ge(s_pv["a"].sem, s_pv["a"].after(n, h - 1))
                dve.tensor_tensor(HIGH[h % 2][:], SIGN[h % 2][:], NOEDGE[:], ALU.is_gt).then_inc(s_w["a"].sem, 1)

            def weights_b(n, p, h):
                if h == 0:
                    if not started(n):
                        dve.wait_ge(folded["c"].sem, folded["c"].after(0, 2))
                    dve.wait_ge(s_diag.sem, s_diag.after(n, 2))
                s, hh = ("b", h) if h < H1 else ("c", 0)
                q = (p + h) % 2
                dve.wait_ge(b_g.free.sem, b_g.free.after(n, h + 2))
                if not (isinstance(n, int) and n == 0 and h < 2):
                    dve.wait_ge(s_pv["b"].sem, s_pv["b"].after(n, h - 1))
                for b in range(NB):
                    ins = dve.scalar_tensor_tensor(W[q][:, b, :], GB[q][:], SC[s][:, b, LO + hh:LO + hh + 1],
                                                   MASK[p][:, b, :], ALU.max, ALU.mult)
                ins.then_inc(s_w["b"].sem, 1)

            def inverse(t, n, k, src, w):
                dve.tensor_scalar(den[t][:, 0:w], src, TINY, None, ALU.max).then_inc(s_den_r[t].sem, 1)
                dve.wait_ge(s_den_r[t].sem, s_den_r[t].after(n, k))
                dve.reciprocal(rden[t][:, 0:w], den[t][:, 0:w]).then_inc(s_rden[t].sem, 1)
                dve.wait_ge(s_rden[t].sem, s_rden[t].after(n, k))

            def outputs0(n, half):
                dve.wait_ge(s_sums.sem, s_sums.after(n, 4 * half + 4))
                if half == 0:
                    dve.wait_ge(s_xm.sem, s_xm.after(n, 1))
                h = slice(4 * half, 4 * half + 4)
                sums = SUMS[:, h].rearrange("p h b c -> p (h b) c")
                inverse("a", n, half + 1, sums[:, :, K0], 4 * NB)
                dve.scalar_tensor_tensor(T[:, h].rearrange("p h b c -> p (h b) c"), sums[:, :, 0:K0], 0.0,
                                         rden["a"][:].unsqueeze(2).to_broadcast([P, 4 * NB, K0]), ALU.max,
                                         ALU.mult).then_inc(s_t.sem, 1)

            def outputs1(n, h):
                for half in range(2):
                    bk = b_o[half]
                    if half == 0:
                        dve.wait_ge(s_half.sem, s_half.after(n, h + 1))
                    else:
                        dve.wait_ge(s_pv["b"].sem, s_pv["b"].after(n, h + 1))
                    sums = bk.t[:, 0:2 * (F1 + 1)].rearrange("p (b c) -> p b c", c=F1 + 1)
                    inverse("b", n, 2 * h + half + 1, sums[:, :, F1], 2)
                    if h:
                        dve.wait_ge(b_m.full.sem, b_m.full.after(n, 3 + h))
                    dve.tensor_tensor(Y[:, 2 * half:2 * half + 2, :], sums[:, :, 0:F1],
                                      rden["b"][:, 0:2].unsqueeze(2).to_broadcast([P, 2, F1]),
                                      ALU.mult).then_inc(bk.free.sem, 1)

            def final(n, blocks):
                if blocks[0] == 0:
                    dve.wait_ge(s_x1b.sem, s_x1b.after(n, 1))
                for b in blocks:
                    bk = b_o[b % 2]
                    if b < NB - 1:
                        dve.wait_ge(s_half.sem, s_half.after(n, H1 + b + 1))
                    else:
                        dve.wait_ge(s_pv["b"].sem, s_pv["b"].after(n, H1 + 1))
                    inverse("b", n, 2 * H1 + b + 1, bk.t[:, F2:F2 + 1], 1)
                    dve.scalar_tensor_tensor(OUT[:, b, :], bk.t[:, 0:F2], rden["b"][:, 0:1], OUT[:, b, :], ALU.mult,
                                             ALU.add).then_inc(s_fin.sem, 1)

            def mask(n, p):
                dve.wait_ge(adj_in.sem, adj_in.after(n, 16))
                dve.tensor_scalar(MASK[p][:], ADJ[:], 0.0, None, ALU.is_gt).then_inc(s_mask.sem, 1)

            def no_edges(n):
                dve.wait_ge(a_m.free.sem, a_m.free.after(n, 5))
                dve.wait_ge(a_g.free.sem, a_g.free.after(n, 1))
                dve.tensor_scalar(NOEDGE[:], MASKT[:], -1.0, 1.0, ALU.mult, ALU.add).then_inc(s_noedge.sem, 1)

            def diagonal(n, p):
                dve.wait_ge(a_g.full.sem, a_g.full.after(n, 1))
                flat = MASK[p][:].rearrange("p b j -> p (b j)")
                step = N + P
                head = flat[:, 0:(NB - 1) * step].rearrange("p (b c) -> p b c", c=step)[:, :, 0:P]
                tail = flat[:, (NB - 1) * step:NB * N]
                dve.tensor_tensor(head, head, identb[:].unsqueeze(1).to_broadcast([P, NB - 1, P]),
                                  ALU.max).then_inc(s_diag.sem, 1)
                dve.tensor_tensor(tail, tail, identb[:], ALU.max).then_inc(s_diag.sem, 1)

            def joint(nb, pb, na, pa, nx, px):
                A, Bt, NX = na is not None, nb is not None, nx is not None
                if Bt:
                    bounds("b", nb, b_m, 2)
                if NX:
                    dve.wait_ge(x_in[px].sem, x_in[px].after(nx, 16 - 8 * px))
                    statistics("a", nx, X[px])
                if Bt:
                    gate_low("b", nb)
                    scalars("b", nb, b_m, 3, V1[:, :, :, F1])
                    values1(nb, 0)
                    values1(nb, 1)
                if A:
                    weights_a(na, 0)
                    weights_a(na, 1)
                if Bt:
                    weights_b(nb, pb, 0)
                    values1(nb, 2)
                    values1(nb, 3)
                if A:
                    lonely(na)
                if A:
                    weights_a(na, 2)
                for h in range(H1):
                    if Bt:
                        if h + 1 < H1:
                            weights_b(nb, pb, h + 1)
                        outputs1(nb, h)
                    if A:
                        weights_a(na, h + 3)
                    if NX and h == 1:
                        mean_shift("a", nx)
                    if h >= 2 and A and not Bt:
                        fold("bc"[h - 2], 0)
                        fold("bc"[h - 2], 1)
                if A:
                    outputs0(na, 0)
                if Bt:
                    elu(nb, 3)
                if A:
                    weights_a(na, 7)
                if NX:
                    if not started(nx):
                        fold("a", 0)
                        fold("a", 1)
                    bounds("a", nx, a_m, 3)
                if Bt:
                    bounds("c", nb, b_o[1], 3)
                    gate_low("c", nb)
                if Bt:
                    scalars("c", nb, b_m, 8, V2[:, :, F2:F2 + 1])
                if A:
                    outputs0(na, 1)
                if Bt:
                    weights_b(nb, pb, H1)
                if A:
                    dve.wait_ge(s_x1.sem, s_x1.after(na, 2))
                    statistics("b", na, X1[pa])
                if NX:
                    gate_low("a", nx)
                    scalars("a", nx, a_m, 4, None)
                if A:
                    mean_shift("b", na)
                if NX:
                    mask(nx, px)
                if Bt:
                    final(nb, (0,))
                if NX:
                    values0(nx, 0)
                if Bt:
                    final(nb, (1,))
                if NX:
                    values0(nx, 1)
                if Bt:
                    final(nb, (2,))
                if NX:
                    rests(nx, 0)
                if Bt:
                    final(nb, (3,))
                if NX:
                    rests(nx, 1)
                    no_edges(nx)
                    low_part(nx, 1)
                    diagonal(nx, px)

            joints(dve, joint)

        @block.tensor
        def _(pe):
            def claim(bk, n, k):
                if started(n, k):
                    pe.wait_ge(bk.free.sem, bk.free.after(n, k))

            def transpose_h(t, n, k, bk, use):
                pe.wait_ge(s_h[t].sem, s_h[t].after(n, NB))
                claim(bk, n, use)
                for b in range(NB):
                    ins = pe.transpose(bk.t[:, b * P:(b + 1) * P], Hn[t][:, b, k * P:(k + 1) * P], ident[:])
                ins.then_inc(bk.full.sem, 1)

            def score_rows(t, n, src, nk, bk, use):
                claim(bk, n, use)
                if not started(n):
                    pe.wait_ge(folded[t].sem, folded[t].after(0, 2))
                for k in range(nk):
                    ins = pe.matmul(bk.t[0:LO + heads[t], :], rows_w[t][:, k, :], src[:, k, :],
                                    start=(k == 0), stop=(k == nk - 1))
                ins.then_inc(bk.full.sem, 1)

            def transpose_scalars(t, n, rows_bank, rows_use, bk, use):
                pe.wait_ge(rows_bank.free.sem, rows_bank.free.after(n, rows_use))
                if t == "a":
                    pe.wait_ge(s_ga.sem, s_ga.after(n, 1))
                claim(bk, n, use)
                for b in range(NB):
                    ins = pe.transpose(bk.t[:, b * P:(b + 1) * P], RT[t][:, b * P:(b + 1) * P], ident[:])
                ins.then_inc(bk.full.sem, 1)

            def project0(n, half):
                bk = a_o[half]
                claim(bk, n, 0)
                for j in range(2):
                    b = 2 * half + j
                    for k in range(KB):
                        ins = pe.matmul(bk.t[:, j * D:(j + 1) * D], HT["a"][:, k, b * P:(b + 1) * P], WP[:, k, :],
                                        start=(k == 0), stop=(k == KB - 1))
                ins.then_inc(bk.full.sem, 1)

            def project1(n, b):
                bk = b_o[b % 2]
                claim(bk, n, b // 2)
                if b < 2 and started(n):
                    pe.wait_ge(s_fin.sem, s_fin.after(n - 1, 3 + b))
                for k in range(KB):
                    ins = pe.matmul(bk.t[:], HT["b"][:, k, b * P:(b + 1) * P], W1[:, k, :],
                                    start=(k == 0), stop=(k == KB - 1))
                ins.then_inc(bk.full.sem, 1)

            def project2(n, half):
                bk = b_o[half]
                claim(bk, n, 6 + half)
                for j in range(2):
                    b = 2 * half + j
                    for k in range(FB):
                        ins = pe.matmul(bk.t[:, j * F2:(j + 1) * F2], GT[:, k, b * P:(b + 1) * P], W2[:, k, :],
                                        start=(k == 0), stop=(k == FB - 1))
                ins.then_inc(bk.full.sem, 1)

            def transpose_mask(n, p):
                pe.wait_ge(s_mask.sem, s_mask.after(n, 1))
                for half, (bk, use) in enumerate(((a_m, 4), (a_g, 0))):
                    claim(bk, n, use)
                    dst = bk.t[:].bitcast(BF16)
                    for jb in range(2):
                        j = 2 * half + jb
                        for b in range(NB):
                            ins = pe.transpose(dst[:, jb * N + b * P:jb * N + (b + 1) * P],
                                               MASK[p][:, b, j * P:(j + 1) * P], identb[:])
                    ins.then_inc(bk.full.sem, 1)

            def mean_row(n):
                claim(a_m, n, 5)
                for k in range(KB):
                    ins = pe.matmul(a_m.t[:, 0:D], hsum[:, k:k + 1].to_broadcast([P, P]), WP[:, k, :],
                                    start=(k == 0), stop=(k == KB - 1))
                ins.then_inc(a_m.full.sem, 1)

            def spread(t, n, h, bk, use):
                w = LO + heads[t]
                claim(bk, n, use)
                pe.wait_ge(s_gl[t].sem, s_gl[t].after(n, 1))
                pe.matmul(bk.t[:], pick[0:w, h, :], GS[t][0:w, :], start=True, stop=True).then_inc(bk.full.sem, 1)

            def spread_a(n, h):
                spread("a", n, h, a_g, 1 + h)

            def spread_b(n, h):
                if h < H1:
                    spread("b", n, h, b_g, 1 + h)
                else:
                    spread("c", n, 0, b_g, 1 + h)

            def all_lows(n, blocks):
                if blocks[0] == 0:
                    pe.wait_ge(s_lo.sem, s_lo.after(n, 2))
                for b in blocks:
                    bk = a_o[b % 2]
                    claim(bk, n, 1 + b // 2)
                    for j in range(NB):
                        for k in range(3):
                            ins = pe.matmul(bk.t[:, 0:H0 * C0], MASKT[:, j, b * P:(b + 1) * P], PARTS[:, k, j, :, 1, :],
                                            start=(j == 0 and k == 0), stop=(j == NB - 1 and k == 2))
                    ins.then_inc(bk.full.sem, 1)

            def sums0(n, h):
                bk = a_o[h % 2]
                claim(bk, n, 3 + h // 2)
                pe.wait_ge(s_w["a"].sem, s_w["a"].after(n, h + 1))
                for b in range(NB):
                    at = b * 2 * C0
                    for j in range(NB):
                        for k in range(3):
                            ins = pe.matmul(bk.t[:, at:at + 2 * C0], HIGH[h % 2][:, j, b * P:(b + 1) * P],
                                            PARTS[:, k, j, h], start=(j == 0 and k == 0), stop=(j == NB - 1 and k == 2))
                ins.then_inc(s_pv["a"].sem, 1)

            def sums1(n, p, h):
                pe.wait_ge(s_w["b"].sem, s_w["b"].after(n, h + 1))
                if h == 0:
                    pe.wait_ge(s_den["b"].sem, s_den["b"].after(n, 1))
                    for o in b_o:
                        pe.wait_ge(o.free.sem, o.free.after(n, 2))
                for b in range(NB):
                    bk = b_o[b // 2]
                    if b % 2 == 0:
                        claim(bk, n, 2 + h)
                    at = (b % 2) * (F1 + 1)
                    for j in range(NB):
                        ins = pe.matmul(bk.t[:, at:at + F1 + 1], W[(p + h) % 2][:, j, b * P:(b + 1) * P],
                                        V1[:, j, h, :], start=(j == 0), stop=(j == NB - 1))
                    if b == 1:
                        ins.then_inc(s_half.sem, 1)
                ins.then_inc(s_pv["b"].sem, 1)

            def sums2(n, p, blocks):
                if blocks[0] == 0:
                    pe.wait_ge(s_w["b"].sem, s_w["b"].after(n, H1 + 1))
                    for o, used in zip(b_o, (7, 8)):
                        pe.wait_ge(o.free.sem, o.free.after(n, used))
                for b in blocks:
                    bk = b_o[b % 2]
                    if b >= 2:
                        pe.wait_ge(s_fin.sem, s_fin.after(n, b - 1))
                    for j in range(NB):
                        ins = pe.matmul(bk.t[:, 0:F2 + 1], W[(p + H1) % 2][:, j, b * P:(b + 1) * P], V2[:, j, :],
                                        start=(j == 0), stop=(j == NB - 1))
                    ins.then_inc(s_half.sem if b < NB - 1 else s_pv["b"].sem, 1)

            def transpose_y(n, h):
                for o in b_o:
                    pe.wait_ge(o.free.sem, o.free.after(n, 3 + h))
                claim(b_m, n, 3 + h)
                for b in range(NB):
                    ins = pe.transpose(b_m.t[:, b * P:(b + 1) * P], Y[:, b, :], ident[:])
                ins.then_inc(b_m.full.sem, 1)

            def joint(nb, pb, na, pa, nx, px):
                A, Bt, NX = na is not None, nb is not None, nx is not None
                if A:
                    spread_a(na, 0)
                if Bt:
                    pe.wait_ge(b_g.free.sem, b_g.free.after(nb, 1))
                    if not started(nb):
                        pe.wait_ge(wb_in.sem, wb_in.after(0, 16 * 8))
                    score_rows("b", nb, HT["b"], KB, b_m, 1)
                    project1(nb, 0)
                    project1(nb, 1)
                if A:
                    all_lows(na, (0, 1))
                if Bt:
                    transpose_scalars("b", nb, b_m, 2, b_m, 2)
                if A:
                    spread_a(na, 1)
                    all_lows(na, (2, 3))
                if Bt:
                    spread_b(nb, 0)
                    project1(nb, 2)
                if A:
                    spread_a(na, 2)
                    sums0(na, 0)
                if Bt:
                    project1(nb, 3)
                if A:
                    sums0(na, 1)
                for h in range(H1):
                    if Bt:
                        if h + 1 < H1:
                            spread_b(nb, h + 1)
                        if h:
                            transpose_y(nb, h - 1)
                    if A:
                        spread_a(na, h + 3)
                    if Bt:
                        sums1(nb, pb, h)
                    if A:
                        sums0(na, h + 2)
                if NX:
                    transpose_h("a", nx, 0, a_m, 0)
                if Bt:
                    transpose_y(nb, H1 - 1)
                if A:
                    spread_a(na, 7)
                if NX:
                    transpose_h("a", nx, 1, a_m, 1)
                if A:
                    sums0(na, 6)
                if NX:
                    score_rows("a", nx, HT["a"], KB, a_m, 2)
                if Bt:
                    pe.wait_ge(s_gt.sem, s_gt.after(nb, H1))
                    score_rows("c", nb, GT, FB, b_o[1], 6)
                    project2(nb, 0)
                if A:
                    sums0(na, 7)
                if Bt:
                    transpose_scalars("c", nb, b_o[1], 7, b_m, 7)
                    spread_b(nb, H1)
                if Bt:
                    project2(nb, 1)
                if NX:
                    project0(nx, 0)
                    project0(nx, 1)
                    transpose_scalars("a", nx, a_m, 3, a_m, 3)
                if Bt:
                    sums2(nb, pb, (0, 1))
                if NX:
                    transpose_mask(nx, px)
                if A:
                    transpose_h("b", na, 0, b_m, 0)
                    transpose_h("b", na, 1, b_g, 0)
                if Bt:
                    sums2(nb, pb, (2, 3))
                if NX:
                    mean_row(nx)

            pe.wait_ge(cst.sem, 11)
            pe.wait_ge(wa_in.sem, wa_in.after(0, 16 * 3))
            joints(pe, joint)


_INS = ['x', 'adj', 'L0_gnn_W_proj', 'L0_gnn_W_att', 'L0_gnn_b_att', 'L1_gnn_W1', 'L1_gnn_att_src1',
        'L1_gnn_att_dst1', 'L1_gnn_b1', 'L1_gnn_W2', 'L1_gnn_att_src2', 'L1_gnn_att_dst2', 'L1_gnn_b2']
_OUTS = [((16, 512, 256), 'float32')]


def kernel(**inputs):
    import numpy as _np
    import concourse.bacc as _bacc
    from concourse import mybir as _mybir
    from concourse.bass_utils import run_bass_kernel_spmd as _run

    nc = _bacc.Bacc("TRN2", target_bir_lowering=False, num_devices=1)
    arrays, args = {}, []
    for name in _INS:
        a = _np.ascontiguousarray(inputs[name])
        arrays[f"in_{name}_dram"] = a
        args.append(nc.dram_tensor(f"in_{name}_dram", a.shape, _mybir.dt.from_np(a.dtype), kind="ExternalInput").ap())
    for i, (shape, dtype) in enumerate(_OUTS):
        dt = _mybir.dt.from_np(_np.dtype(dtype))
        args.append(nc.dram_tensor(f"out_{i}_dram", shape, dt, kind="ExternalOutput").ap())
    gnn_kernel(nc, *args)
    r = _run(nc, [arrays], core_ids=[0])
    got = tuple(r.results[0][f"out_{i}_dram"] for i in range(len(_OUTS)))
    return got[0]
```

```python
from contextlib import ExitStack

import concourse.bass as bass
from concourse import mybir

ALU = mybir.AluOpType
ACT = mybir.ActivationFunctionType
AX_X = mybir.AxisListType.X
F32 = mybir.dt.float32
F32R = mybir.dt.float32r
BF16 = mybir.dt.bfloat16
I32 = mybir.dt.int32

P = 128
LO = 32
SLOPE = 0.2
EPS = 1e-5
LIFT = 60.0
TINY = 1e-37


class Signal:

    def __init__(self, sem, per_batch):
        self.sem, self.per_batch = sem, per_batch

    def after(self, n, k):
        return self.per_batch * n + k


class Bank:

    def __init__(self, tensor, full, free):
        self.t, self.full, self.free = tensor, full, free


def started(n, k=0):
    return not (isinstance(n, int) and n == 0 and k == 0)


def gnn_kernel(nc, x, adj, w_proj, w_att, b_att, w1, att_src1, att_dst1, b1, w2, att_src2, att_dst2, b2, out):
    B, N, D = x.shape
    H0, K2 = w_att.shape
    K0 = K2 // 2
    H1, F1 = att_src1.shape
    F2 = att_src2.shape[1]
    NB = N // P
    KB = D // P
    FB = H1 * F1 // P
    assert F1 == P and H0 * K0 == D and F2 == D and H0 % 4 == 0 and N == 512 and B % 2 == 0

    with ExitStack() as ctx:
        def sb(name, shape, dt=F32):
            return ctx.enter_context(nc.sbuf_tensor(name, shape, dt))

        def signal(name, per_batch=1):
            return Signal(ctx.enter_context(nc.semaphore(name)), per_batch)

        def bank(name, full, free):
            return Bank(ctx.enter_context(nc.psum_tensor(name, [P, 512], F32)),
                        signal(name + "_full", full), signal(name + "_free", free))

        a_m = bank("a_m", 6, 6)
        a_o = [bank("a_o0", 3, 7), bank("a_o1", 3, 7)]
        a_g = bank("a_g", 1 + H0, 1 + H0)
        b_m = bank("b_m", 5 + H1, 5 + H1)
        b_g = bank("b_g", H1 + 2, H1 + 2)
        b_o = [bank("b_o0", 3, 7), bank("b_o1", 3, 7)]

        WP = sb("WP", [P, KB, D])
        W_high = {"b": sb("W1_high", [P, KB, H1 * F1], F32R), "c": sb("W2_high", [P, FB, F2], F32R)}
        W_low = {"b": sb("W1_low", [P, KB, H1 * F1], F32R), "c": sb("W2_low", [P, FB, F2], F32R)}
        C0 = K0 + 1
        rest_store = sb("rest_store", [P, NB * H0 * 2 * C0])
        REST = rest_store[:].rearrange("p (b h u c) -> p b h u c", b=NB, h=H0, u=2)
        XN = rest_store[:, 0:NB * D].rearrange("p (b d) -> p b d", b=NB)
        XM = rest_store[:, NB * D:2 * NB * D].rearrange("p (b d) -> p b d", b=NB)
        v0_store = sb("v0_store", [P, NB * H0 * 2 * C0])
        V0 = v0_store[:].rearrange("p (b h u c) -> p b h u c", b=NB, h=H0, u=2)
        SUMS = v0_store[:, 0:H0 * NB * C0].rearrange("p (h b c) -> p h b c", h=H0, b=NB)
        T = v0_store[:, H0 * NB * C0:H0 * NB * (C0 + K0)].rearrange("p (h b c) -> p h b c", h=H0, b=NB)
        rows_w = {"a": sb("rows_w0", [P, KB, LO + H0]), "b": sb("rows_w1", [P, KB, LO + H1]),
                  "c": sb("rows_w2", [P, FB, LO + 1])}
        rows_w_high = {"b": sb("rows_w1_high", [P, KB, LO + H1], F32R), "c": sb("rows_w2_high", [P, FB, LO + 1], F32R)}
        rows_w_low = {"b": sb("rows_w1_low", [P, KB, LO + H1], F32R), "c": sb("rows_w2_low", [P, FB, LO + 1], F32R)}
        batt = sb("batt", [H0, 1])
        b1c = sb("b1c", [P, H1])
        b2r = sb("b2r", [P, F2])
        ident = sb("ident", [P, P])
        identb = sb("identb", [P, P], BF16)
        pick32 = sb("pick32", [LO + H0, H0])
        pick = sb("pick", [LO + H0, H0], F32R)
        lift = sb("lift", [P, 1])
        one = sb("one", [P, 1])
        b1n = sb("b1n", [P, H1])
        power = sb("power", [P, NB])
        warm = sb("warm", [P, 1])

        X = [sb(f"X{p}", [P, NB, D]) for p in range(2)]
        ADJ = sb("ADJ", [P, NB, N], I32)
        MASK = [sb(f"MASK{p}", [P, NB, N], BF16) for p in range(2)]
        MASKT = sb("MASKT", [P, NB, N], BF16)
        NOEDGE = sb("NOEDGE", [P, NB, N], BF16)
        X1 = [sb(f"X1{p}", [P, NB, D]) for p in range(2)]
        OUT = sb("OUT", [P, NB, F2])
        RM = sb("RM", [P, D])
        hsum = sb("hsum", [P, KB])
        none = sb("none", [P, NB])
        stats = {t: sb("stats_" + t, [P, NB, 6]) for t in "ab"}
        mv = {t: sb("mv_" + t, [P, NB, 5]) for t in "ab"}
        veps = {t: sb("veps_" + t, [P, NB]) for t in "ab"}
        rstd = {t: sb("rstd_" + t, [P, NB]) for t in "ab"}
        shift = {t: sb("shift_" + t, [P, NB]) for t in "ab"}
        y_store = sb("y_store", [P, 3 * NB * F1])
        Y = y_store[:, 0:NB * F1].rearrange("p (b c) -> p b c", b=NB)
        EX = y_store[:, NB * F1:NB * F1 + N]
        RL = y_store[:, NB * F1 + N:NB * F1 + 2 * N]
        Hn = {"a": XN, "b": y_store[:, 0:NB * D].rearrange("p (b d) -> p b d", b=NB)}
        GT = [sb("GT_high", [P, FB, N], F32R), sb("GT_low", [P, FB, N], F32R)]
        HT_a = sb("HT_a", [P, KB, N])
        HT_b = [g[:, 0:KB] for g in GT]
        heads = {"a": H0, "b": H1, "c": 1}
        top = {t: sb("top_" + t, [LO + H0, 1]) for t in "abc"}
        atop = {t: sb("atop_" + t, [H0, 1]) for t in "abc"}
        top8 = {t: sb("top8_" + t, [LO + H0, 1]) for t in "abc"}
        top2 = {t: sb("top2_" + t, [LO + H0, 1]) for t in "abc"}
        top2lo = {t: sb("top2lo_" + t, [H0, 1]) for t in "abc"}
        Z = {"a": sb("Z_a", [H0, N]), "b": sb("Z_b", [H1, N])}
        GS = {"a": sb("GS_a", [LO + H0, N], F32R), "b": sb("GS_b", [LO + H1, N], F32R)}
        RT = {"a": sb("RT_a", [P, N]), "b": sb("RT_b", [P, N])}
        for rows in (Z, GS, RT):
            rows["c"] = rows["b"]
        SC = {t: sb("SC_" + t, [P, NB, (2 * LO if t == "a" else LO) + heads[t]]) for t in "abc"}
        PARTS = sb("PARTS", [P, 3, NB, H0, 2, C0], BF16)
        SIGN = [sb(f"SIGN{q}", [P, NB, N], BF16) for q in range(2)]
        HIGH = [sb(f"HIGH{q}", [P, NB, N], BF16) for q in range(2)]
        MS = sb("MS", [P, NB, H0, C0])
        SS = [sb(f"SS{q}", [P, NB, 2, C0]) for q in range(2)]
        LOWS = sb("LOWS", [P, NB, C0])
        GLOWS = sb("GLOWS", [P, NB, C0])
        V1 = sb("V1", [P, NB, H1, F1 + 1])
        w_store = V1[:].rearrange("p b h c -> p (b h c)")
        W1 = w_store[:, 0:KB * H1 * F1].rearrange("p (k o) -> p k o", k=KB)
        W2 = w_store[:, KB * H1 * F1:KB * H1 * F1 + FB * F2].rearrange("p (k o) -> p k o", k=FB)
        V2 = V1[:].rearrange("p b h c -> p (b h c)")[:, 0:NB * (F2 + 1)].rearrange("p (b c) -> p b c", b=NB)
        GB = [sb(f"GB{q}", [P, N]) for q in range(2)]
        W = [sb(f"weights{q}", [P, NB, N]) for q in range(2)]
        att_store, prod = (w[:].rearrange("p b i -> p (b i)") for w in W)
        att0 = att_store[:, 0:H0 * K2].rearrange("p (h c) -> p h c", h=H0)
        att1 = att_store[:, 512:1536].rearrange("p (s h c) -> p s h c", s=2, h=H1)
        att2 = att_store[:, 1536:2048].rearrange("p (s c) -> p s c", s=2)
        den = {t: sb("den_" + t, [P, 16]) for t in "ab"}
        rden = {t: sb("rden_" + t, [P, 16]) for t in "ab"}

        wa_in = signal("weights_in_a", 16 * 3)
        wb_in = signal("weights_in_b", 16 * 8)
        folded = {t: signal("folded_" + t, 2) for t in "abc"}
        split_w = {t: signal("weights_split_" + t, 4) for t in "bc"}
        s_hth = signal("ht_high_b", KB)
        s_el = signal("elu_steps_dve", 2 * (H1 - 1))
        cst = signal("cst")
        cst_b = signal("cst_b")
        setup = signal("setup")
        x_in = [signal(f"x_in{p}", 8) for p in range(2)]
        adj_in = signal("adj_in", 16)
        s_bn = {t: signal("bn_" + t, NB) for t in "ab"}
        s_mv = {t: signal("mv_done_" + t, 5) for t in "ab"}
        s_ve = {t: signal("veps_done_" + t) for t in "ab"}
        s_rstd = {t: signal("rstd_done_" + t) for t in "ab"}
        s_shift = {t: signal("shift_done_" + t) for t in "ab"}
        s_h = {t: signal("h_done_" + t, NB) for t in "ab"}
        s_top = {t: signal("top_done_" + t) for t in "abc"}
        s_small = {t: signal("small_done_" + t, 4) for t in "abc"}
        s_z = {t: signal("z_done_" + t) for t in "abc"}
        s_g = {t: signal("g_done_" + t) for t in "abc"}
        s_ga = signal("gates_to_transpose")
        s_gh = {t: signal("g_high_" + t) for t in "abc"}
        s_gl = {t: signal("g_low_" + t) for t in "abc"}
        s_den = {t: signal("den_col_" + t) for t in "abc"}
        s_mask = signal("mask_done")
        s_diag = signal("diag_done", 2)
        s_noedge = signal("noedge_done")
        s_w = {"a": signal("weights_a", H0), "b": signal("weights_b", H1 + 1)}
        s_pv = {"a": signal("sums_a", H0), "b": signal("sums_b", H1 + 1)}
        s_half = signal("half_sums_b", H1 + NB - 1)
        s_den_r = {"a": signal("den_a", 2), "b": signal("den_b", 2 * H1 + NB)}
        s_rden = {"a": signal("rden_a", 2), "b": signal("rden_b", 2 * H1 + NB)}
        s_none = signal("none_done")
        s_xn = signal("xn_done")
        s_xm = signal("xm_done")
        s_u = signal("u_done", 2)
        s_hi = signal("high_part", 2)
        s_rest = [signal(f"rest_done{half}") for half in range(2)]
        s_mid = signal("middle_part", 2)
        s_lo = signal("low_part", 2)
        s_lows = signal("lows_done", H0)
        s_glows = signal("glows_done", H0)
        s_sums = signal("sums_done", H0)
        s_t = signal("outputs_a", 2)
        s_x1 = signal("x1_done", 2)
        s_ex = signal("exp_done", H1)
        s_em = signal("elu_steps_pool", 3)
        s_gt = signal("gt_done", H1)
        s_x1b = signal("x1b_done")
        s_fin = signal("fin_done", NB)
        s_out = signal("out_done", 16)

        block = ctx.enter_context(nc.Block())

        @block.sync
        def _(sp):
            def load(n, p):
                if started(n) and not (isinstance(n, int) and n < 2):
                    sp.wait_ge(s_xm.sem, s_xm.after(n - 2, 1))
                sp.dma_start(X[p][:], x[n].rearrange("(b p) d -> p b d", p=P)).then_inc(x_in[p].sem, 16)
                if started(n):
                    sp.wait_ge(s_mask.sem, s_mask.after(n - 1, 1))
                sp.dma_start(ADJ[:], adj[n].rearrange("(b p) j -> p b j", p=P)).then_inc(adj_in.sem, 16)

            def store(n):
                sp.wait_ge(s_fin.sem, s_fin.after(n, NB))
                sp.dma_start(out[n].rearrange("(b p) d -> p b d", p=P), OUT[:]).then_inc(s_out.sem, 16)

            load(0, 0)
            for dst, src, done in (
                (WP[:], w_proj.rearrange("(k p) o -> p k o", p=P), wa_in),
                (att0, w_att.partition_broadcast(P), wa_in),
                (batt[:], b_att.rearrange("(h a) -> h a", a=1), wa_in),
                (W1, w1.rearrange("(k p) o -> p k o", p=P), wb_in),
                (W2, w2.rearrange("(k p) o -> p k o", p=P), wb_in),
                (att1[:, 0], att_dst1.partition_broadcast(P), wb_in),
                (att1[:, 1], att_src1.partition_broadcast(P), wb_in),
                (att2[:, 0], att_dst2[0].partition_broadcast(P), wb_in),
                (att2[:, 1], att_src2[0].partition_broadcast(P), wb_in),
                (b2r[:], b2.partition_broadcast(P), wb_in),
                (b1c[:], b1.rearrange("(h p) -> p h", p=P), wb_in),
            ):
                with nc.allow_non_contiguous_dma(reason="two short vectors, once"):
                    sp.dma_start(dst, src).then_inc(done.sem, 16)
            load(1, 1)
            load(2, 0)
            with sp.Fori(0, B // 2 - 2) as i:
                for p in range(2):
                    load(2 * i + 3 + p, 1 - p)
                    store(2 * i + p)
            load(B - 1, 1)
            for n in range(B - 4, B):
                store(n)
            sp.wait_ge(s_out.sem, s_out.after(B - 1, 16))

        def joints(engine, joint):
            joint(None, None, None, None, 0, 0)
            joint(None, None, 0, 0, 1, 1)
            joint(0, 0, 1, 1, 2, 0)
            with engine.Fori(0, B // 2 - 2) as i:
                joint(2 * i + 1, 1, 2 * i + 2, 0, 2 * i + 3, 1)
                joint(2 * i + 2, 0, 2 * i + 3, 1, 2 * i + 4, 0)
            joint(B - 3, 1, B - 2, 0, B - 1, 1)
            joint(B - 2, 0, B - 1, 1, None, None)
            joint(B - 1, 1, None, None, None, None)

        @block.gpsimd
        def _(pool):
            pool.memset(ident[:], 0.0).then_inc(cst.sem, 1)
            pool.memset(pick32[:], 0.0).then_inc(cst.sem, 1)
            pool.memset(lift[:], LIFT).then_inc(cst.sem, 1)
            pool.memset(power[:], -0.5).then_inc(cst.sem, 1)
            pool.memset(one[:], 1.0).then_inc(cst.sem, 1)
            pool.wait_ge(cst.sem, 5)
            pool.affine_select(out=ident[:], in_=ident[:], compare_op=ALU.not_equal, fill=1.0, base=0,
                               pattern=[[-1, P]], channel_multiplier=1).then_inc(cst.sem, 1)
            pool.affine_select(out=pick32[:], in_=pick32[:], compare_op=ALU.not_equal, fill=1.0, base=0,
                               pattern=[[-1, H0]], channel_multiplier=1).then_inc(cst.sem, 1)
            pool.wait_ge(cst.sem, 7)
            pool.affine_select(out=pick32[:], in_=pick32[:], compare_op=ALU.not_equal, fill=1.0, base=-LO,
                               pattern=[[-1, H0]], channel_multiplier=1).then_inc(cst.sem, 1)
            pool.tensor_copy(identb[:], ident[:]).then_inc(cst.sem, 1)
            for t in "ab":
                pool.memset(RT[t][:], 0.0).then_inc(cst.sem, 1)
            pool.wait_ge(cst.sem, 11)

            def rstd_of(t, n):
                pool.wait_ge(s_ve[t].sem, s_ve[t].after(n, 1))
                pool.tensor_tensor(rstd[t][:], veps[t][:], power[:], ALU.pow).then_inc(s_rstd[t].sem, 1)

            def elu(n, h):
                pool.wait_ge(s_ex.sem, s_ex.after(n, h + 1))
                pool.tensor_tensor(EX, EX, one[:].to_broadcast([P, N]), ALU.subtract).then_inc(s_em.sem, 1)
                pool.wait_ge(s_em.sem, s_em.after(n, 3 * h + 1))
                pool.tensor_tensor(GT[0][:, h, :], EX, RL, ALU.add).then_inc(s_em.sem, 1)
                pool.wait_ge(s_em.sem, s_em.after(n, 3 * h + 2))
                pool.tensor_tensor(EX, EX, GT[0][:, h, :].bitcast(F32), ALU.subtract).then_inc(s_em.sem, 1)
                pool.wait_ge(s_em.sem, s_em.after(n, 3 * h + 3))
                pool.tensor_tensor(GT[1][:, h, :], EX, RL, ALU.add).then_inc(s_gt.sem, 1)

            def rest(n):
                pool.wait_ge(s_hi.sem, s_hi.after(n, 1))
                pool.tensor_tensor(REST[:, 0:2], V0[:, 0:2], PARTS[:, 0, 0:2], ALU.subtract).then_inc(s_rest[0].sem, 1)

            def low_part(n, half):
                pool.wait_ge(s_mid.sem, s_mid.after(n, half + 1))
                b = slice(2 * half, 2 * half + 2)
                pool.tensor_tensor(PARTS[:, 2, b], REST[:, b], PARTS[:, 1, b], ALU.subtract).then_inc(s_lo.sem, 1)

            def x_and_mean(n, p):
                pool.wait_ge(s_none.sem, s_none.after(n, 1))
                pool.tensor_tensor(XN, RM[:].unsqueeze(1).to_broadcast([P, NB, D]),
                                   none[:].unsqueeze(2).to_broadcast([P, NB, D]), ALU.mult).then_inc(s_xn.sem, 1)
                pool.wait_ge(s_xn.sem, s_xn.after(n, 1))
                pool.tensor_tensor(XM, XN, X[p][:], ALU.add).then_inc(s_xm.sem, 1)

            def combine(n, h):
                pool.wait_ge(a_o[h % 2].free.sem, a_o[h % 2].free.after(n, 4 + h // 2))
                pool.tensor_tensor(LOWS[:], MS[:, :, h], SS[h % 2][:, :, 1], ALU.subtract).then_inc(s_lows.sem, 1)
                pool.wait_ge(s_lows.sem, s_lows.after(n, h + 1))
                pool.tensor_tensor(GLOWS[:], LOWS[:], SC["a"][:, :, 2 * LO + h:2 * LO + h + 1].to_broadcast([P, NB, C0]),
                                   ALU.mult).then_inc(s_glows.sem, 1)
                pool.wait_ge(s_glows.sem, s_glows.after(n, h + 1))
                pool.tensor_tensor(SUMS[:, h], GLOWS[:], SS[h % 2][:, :, 0], ALU.add).then_inc(s_sums.sem, 1)

            def x1(n, p, half):
                pool.wait_ge(s_t.sem, s_t.after(n, half + 1))
                h = slice(4 * half, 4 * half + 4)
                pool.tensor_tensor(X1[p][:].rearrange("p b (h c) -> p h b c", c=K0)[:, h], T[:, h],
                                   XM.rearrange("p b (h c) -> p h b c", c=K0)[:, h], ALU.add).then_inc(s_x1.sem, 1)

            def x1b(n, p):
                if started(n):
                    pool.wait_ge(s_out.sem, s_out.after(n - 1, 16))
                pool.tensor_tensor(OUT[:], X1[p][:], b2r[:].unsqueeze(1).to_broadcast([P, NB, F2]),
                                   ALU.add).then_inc(s_x1b.sem, 1)

            def joint(nb, pb, na, pa, nx, px):
                A, Bt, NX = na is not None, nb is not None, nx is not None
                if Bt:
                    if not started(nb):
                        pool.wait_ge(wb_in.sem, wb_in.after(0, 16 * 8))
                    x1b(nb, pb)
                if NX:
                    rstd_of("a", nx)
                if A:
                    x_and_mean(na, pa)
                    combine(na, 0)
                for h in range(H1):
                    if Bt and h == 1:
                        elu(nb, 0)
                    if A:
                        combine(na, h + 1)
                if A:
                    x1(na, pa, 0)
                    combine(na, 5)
                    combine(na, 6)
                    combine(na, 7)
                    x1(na, pa, 1)
                    rstd_of("b", na)
                if NX:
                    rest(nx)
                    low_part(nx, 0)

            joints(pool, joint)

        @block.scalar
        def _(act):
            act.wait_ge(cst.sem, 11)
            act.activation(warm[:], one[:], ACT.Exp)

            def normalize(t, n, src, blocks):
                act.wait_ge(s_shift[t].sem, s_shift[t].after(n, 1))
                if t == "a" and started(n):
                    act.wait_ge(s_xm.sem, s_xm.after(n - 1, 1))
                for b in blocks:
                    act.activation(Hn[t][:, b, :], src[:, b, :], ACT.Relu, bias=shift[t][:, b:b + 1],
                                   scale=rstd[t][:, b:b + 1]).then_inc(s_h[t].sem, 1)

            def h_transposed(t, n, k, bk, use):
                act.wait_ge(bk.full.sem, bk.full.after(n, use))
                if t == "a":
                    act.activation(HT_a[:, k, :], bk.t[:], ACT.Copy, accum_out=hsum[:, k:k + 1]).then_inc(bk.free.sem, 1)
                else:
                    act.activation(HT_b[0][:, k, :], bk.t[:], ACT.Copy).then_inc(s_hth.sem, 1)

            def row_exps(t, n, bk, use):
                nh = heads[t]
                act.wait_ge(s_small[t].sem, s_small[t].after(n, 4))
                act.activation(RT[t][LO:LO + nh, :], bk.t[LO:LO + nh, :], ACT.Exp, bias=top8[t][LO:LO + nh, :],
                               scale=1.0 - SLOPE)
                act.wait_ge(s_z[t].sem, s_z[t].after(n, 1))
                act.activation(RT[t][0:nh, :], bk.t[LO:LO + nh, :], ACT.Exp, bias=top2[t][LO:LO + nh, :],
                               scale=SLOPE).then_inc(bk.free.sem, 1)
                if t == "a":
                    act.activation(RT[t][2 * LO:2 * LO + nh, :], Z[t][0:nh, :], ACT.Exp, bias=lift[0:nh, :],
                                   scale=SLOPE - 1.0).then_inc(s_ga.sem, 1)
                act.activation(Z[t][0:nh, :], Z[t][0:nh, :], ACT.Exp, bias=lift[0:nh, :],
                               scale=SLOPE - 1.0).then_inc(s_g[t].sem, 1)
                act.wait_ge(s_g[t].sem, s_g[t].after(n, 1))
                act.activation(GS[t][0:nh, :], Z[t][0:nh, :], ACT.Copy).then_inc(s_gh[t].sem, 1)

            def mask_transposed(n):
                for half, (bk, use) in enumerate(((a_m, 5), (a_g, 1))):
                    act.wait_ge(bk.full.sem, bk.full.after(n, use))
                    act.activation(MASKT[:, 2 * half:2 * half + 2, :],
                                   bk.t[:].bitcast(BF16).rearrange("p (b i) -> p b i", b=2),
                                   ACT.Copy).then_inc(bk.free.sem, 1)

            def high_parts(n, half):
                act.wait_ge(s_u.sem, s_u.after(n, half + 1))
                b = slice(2 * half, 2 * half + 2)
                act.activation(PARTS[:, 0, b], V0[:, b], ACT.Copy).then_inc(s_hi.sem, 1)

            def middle_parts(n, half):
                act.wait_ge(s_rest[half].sem, s_rest[half].after(n, 1))
                b = slice(2 * half, 2 * half + 2)
                act.activation(PARTS[:, 1, b], REST[:, b], ACT.Copy).then_inc(s_mid.sem, 1)

            def all_lows(n, blocks):
                if started(n) and blocks[0] == 0:
                    act.wait_ge(s_sums.sem, s_sums.after(n - 1, H0))
                for b in blocks:
                    bk = a_o[b % 2]
                    act.wait_ge(bk.full.sem, bk.full.after(n, 2 + b // 2))
                    act.activation(MS[:, b], bk.t[:, 0:H0 * C0].rearrange("p (h c) -> p h c", c=C0),
                                   ACT.Copy).then_inc(bk.free.sem, 1)

            def signs(n, h):
                act.wait_ge(a_g.full.sem, a_g.full.after(n, h + 2))
                if h == 0:
                    act.wait_ge(a_m.free.sem, a_m.free.after(n, 4))
                if not (isinstance(n, int) and n == 0 and h < 2):
                    act.wait_ge(s_w["a"].sem, s_w["a"].after(n, h - 1))
                for b in range(NB):
                    ins = act.activation(SIGN[h % 2][:, b, :], a_g.t[:], ACT.Sign, scale=-1.0,
                                         bias=SC["a"][:, b, LO + h:LO + h + 1])
                ins.then_inc(a_g.free.sem, 1)

            def head_sums(n, h):
                bk = a_o[h % 2]
                act.wait_ge(s_pv["a"].sem, s_pv["a"].after(n, h + 1))
                if not (isinstance(n, int) and n == 0 and h < 2):
                    act.wait_ge(s_sums.sem, s_sums.after(n, h - 1))
                act.activation(SS[h % 2][:], bk.t[:, 0:NB * 2 * C0].rearrange("p (b u c) -> p b u c", b=NB, u=2),
                               ACT.Copy).then_inc(bk.free.sem, 1)

            def mean_row(n):
                act.wait_ge(a_m.full.sem, a_m.full.after(n, 6))
                act.activation(RM[:], a_m.t[:, 0:D], ACT.Relu, scale=1.0 / N).then_inc(a_m.free.sem, 1)

            def gates_b(n, p, h):
                q = (p + h) % 2
                act.wait_ge(b_g.full.sem, b_g.full.after(n, h + 2))
                if not (isinstance(n, int) and n == 0 and h < 2):
                    act.wait_ge(s_w["b"].sem, s_w["b"].after(n, h - 1))
                act.activation(GB[q][:], b_g.t[:], ACT.Copy).then_inc(b_g.free.sem, 1)

            def elu_parts(n, h):
                act.wait_ge(b_m.full.sem, b_m.full.after(n, 4 + h))
                if started(n, h):
                    act.wait_ge(s_gt.sem, s_gt.after(n, h))
                act.activation(RL, b_m.t[:], ACT.Relu, bias=b1c[:, h:h + 1])
                act.activation(EX, b_m.t[:], ACT.Relu, bias=b1n[:, h:h + 1], scale=-1.0).then_inc(b_m.free.sem, 1)
                act.wait_ge(b_m.free.sem, b_m.free.after(n, 4 + h))
                act.activation(EX, EX, ACT.Exp, scale=-1.0).then_inc(s_ex.sem, 1)

            def values2(n, half):
                bk = b_o[half]
                act.wait_ge(s_den["c"].sem, s_den["c"].after(n, 1))
                act.wait_ge(bk.full.sem, bk.full.after(n, 3))
                for j in range(2):
                    b = 2 * half + j
                    ins = act.activation(V2[:, b, 0:F2], bk.t[:, j * F2:(j + 1) * F2], ACT.Copy,
                                         scale=SC["c"][:, b, 0:1])
                ins.then_inc(bk.free.sem, 1)

            def joint(nb, pb, na, pa, nx, px):
                A, Bt, NX = na is not None, nb is not None, nx is not None
                if Bt:
                    if not started(nb):
                        act.wait_ge(wb_in.sem, wb_in.after(0, 16 * 8))
                        act.wait_ge(cst_b.sem, 2)
                    row_exps("b", nb, b_m, 2)
                if A:
                    mean_row(na)
                    signs(na, 0)
                    all_lows(na, (0, 1))
                    signs(na, 1)
                    all_lows(na, (2, 3))
                if Bt:
                    gates_b(nb, pb, 0)
                if A:
                    signs(na, 2)
                    head_sums(na, 0)
                for h in range(H1):
                    if Bt and h + 1 < H1:
                        gates_b(nb, pb, h + 1)
                    if NX and h == 2:
                        act.wait_ge(x_in[px].sem, x_in[px].after(nx, 16 - 8 * px))
                        normalize("a", nx, X[px], (0, 1))
                    if Bt and h >= 1:
                        elu_parts(nb, h - 1)
                    if A:
                        head_sums(na, h + 1)
                        signs(na, h + 3)
                    if NX and h == 2:
                        normalize("a", nx, X[px], (2, 3))
                if NX:
                    h_transposed("a", nx, 0, a_m, 1)
                if Bt:
                    elu_parts(nb, 3)
                if NX:
                    h_transposed("a", nx, 1, a_m, 2)
                if A:
                    head_sums(na, 5)
                    signs(na, 7)
                    head_sums(na, 6)
                if NX:
                    row_exps("a", nx, a_m, 3)
                if Bt:
                    row_exps("c", nb, b_m, 8)
                if Bt:
                    gates_b(nb, pb, H1)
                    values2(nb, 0)
                if A:
                    head_sums(na, 7)
                if Bt:
                    values2(nb, 1)
                if A:
                    normalize("b", na, X1[pa], range(NB))
                if NX:
                    high_parts(nx, 0)
                if A:
                    h_transposed("b", na, 0, b_m, 1)
                    h_transposed("b", na, 1, b_g, 1)
                if NX:
                    high_parts(nx, 1)
                    mask_transposed(nx)
                    middle_parts(nx, 0)
                    middle_parts(nx, 1)

            joints(act, joint)

        @block.vector
        def _(dve):
            dve.memset(rows_w["a"][:], 0.0)
            dve.memset(rows_w["b"][:], 0.0)
            dve.memset(rows_w["c"][:], 0.0).then_inc(setup.sem, 1)
            for t in "ab":
                dve.memset(GS[t][:].bitcast(F32), 0.0).then_inc(setup.sem, 1)
            dve.wait_ge(cst.sem, 11)
            dve.tensor_copy(pick[:], pick32[:]).then_inc(cst_b.sem, 1)
            dve.wait_ge(setup.sem, 3)

            def fold(t, s):
                w, att, nh = {"a": (WP, att0[:, :, s * K0:(s + 1) * K0], H0), "b": (W1, att1[:, s], H1),
                              "c": (W2, att2[:, s:s + 1], 1)}[t]
                w = w[:, :, :].rearrange("p k (h c) -> p k h c", h=nh)
                nk, c = w.shape[1], w.shape[3]
                pr = prod[:, s * 1024:s * 1024 + nk * nh * c].rearrange("p (k h c) -> p k h c", k=nk, h=nh)
                if t != "a" and s == 0:
                    before = folded["abc"["abc".index(t) - 1]]
                    dve.wait_ge(before.sem, before.after(0, 2))
                if t == "a" and s == 0:
                    dve.wait_ge(wa_in.sem, wa_in.after(0, 16 * 3))
                if t == "b" and s == 0:
                    dve.wait_ge(wb_in.sem, wb_in.after(0, 16 * 8))
                    dve.tensor_scalar(b1n[:], b1c[:], -1.0, None, ALU.mult).then_inc(cst_b.sem, 1)
                dve.tensor_tensor(pr, w, att.unsqueeze(1).to_broadcast([P, nk, nh, c]), ALU.mult).then_inc(setup.sem, 1)
                dve.wait_ge(setup.sem, 4 + 2 * "abc".index(t) + s)
                dve.tensor_reduce(rows_w[t][:, :, s * LO:s * LO + nh], pr, AX_X, ALU.add).then_inc(folded[t].sem, 1)

            def split_weights(t):
                w, w32 = (W1, W2)["bc".index(t)], rows_w[t]
                dve.wait_ge(folded[t].sem, folded[t].after(0, 2))
                dve.tensor_copy(W_high[t][:], w).then_inc(split_w[t].sem, 1)
                dve.tensor_copy(rows_w_high[t][:], w32[:]).then_inc(split_w[t].sem, 1)
                dve.wait_ge(split_w[t].sem, split_w[t].after(0, 2))
                dve.tensor_tensor(W_low[t][:], w, W_high[t][:].bitcast(F32), ALU.subtract).then_inc(split_w[t].sem, 1)
                dve.tensor_tensor(rows_w_low[t][:], w32[:], rows_w_high[t][:].bitcast(F32),
                                  ALU.subtract).then_inc(split_w[t].sem, 1)

            def statistics(t, n, src):
                for b in range(NB):
                    dve.bn_stats(stats[t][:, b, :], src[:, b, :]).then_inc(s_bn[t].sem, 1)
                dve.wait_ge(s_bn[t].sem, s_bn[t].after(n, NB))
                even, odd = stats[t][:, :, 0:3], stats[t][:, :, 3:6]
                dve.tensor_tensor(mv[t][:, :, 0], even[:, :, 1], odd[:, :, 1], ALU.add).then_inc(s_mv[t].sem, 1)
                dve.tensor_tensor(mv[t][:, :, 1], even[:, :, 1], odd[:, :, 1], ALU.subtract).then_inc(s_mv[t].sem, 1)
                dve.tensor_tensor(mv[t][:, :, 2], even[:, :, 2], odd[:, :, 2], ALU.add).then_inc(s_mv[t].sem, 1)
                dve.wait_ge(s_mv[t].sem, s_mv[t].after(n, 3))
                dve.scalar_tensor_tensor(mv[t][:, :, 3], mv[t][:, :, 1], 0.25, mv[t][:, :, 1], ALU.mult,
                                         ALU.mult).then_inc(s_mv[t].sem, 1)
                dve.tensor_scalar(mv[t][:, :, 4], mv[t][:, :, 2], 1.0 / D, EPS, ALU.mult,
                                  ALU.add).then_inc(s_mv[t].sem, 1)
                dve.wait_ge(s_mv[t].sem, s_mv[t].after(n, 5))
                if started(n):
                    dve.wait_ge(s_h[t].sem, s_h[t].after(n - 1, NB))
                dve.tensor_tensor(veps[t][:], mv[t][:, :, 3], mv[t][:, :, 4], ALU.add).then_inc(s_ve[t].sem, 1)

            def mean_shift(t, n):
                dve.wait_ge(s_rstd[t].sem, s_rstd[t].after(n, 1))
                dve.scalar_tensor_tensor(shift[t][:], mv[t][:, :, 0], -0.5, rstd[t][:], ALU.mult,
                                         ALU.mult).then_inc(s_shift[t].sem, 1)

            def bounds(t, n, bk, use):
                nh = heads[t]
                dve.wait_ge(bk.full.sem, bk.full.after(n, use))
                dve.tensor_reduce(top[t][LO:LO + nh, :], bk.t[LO:LO + nh, :], AX_X, ALU.max).then_inc(s_top[t].sem, 1)
                dve.wait_ge(s_top[t].sem, s_top[t].after(n, 1))
                if t == "a":
                    dve.tensor_copy(top2lo[t][0:nh, :], top[t][LO:LO + nh, :]).then_inc(s_small[t].sem, 1)
                    dve.wait_ge(s_small[t].sem, s_small[t].after(n, 1))
                    dve.tensor_tensor(atop[t][0:nh, :], top2lo[t][0:nh, :], batt[:], ALU.add).then_inc(s_small[t].sem, 1)
                else:
                    dve.tensor_copy(atop[t][0:nh, :], top[t][LO:LO + nh, :]).then_inc(s_small[t].sem, 2)
                dve.tensor_scalar(top8[t][LO:LO + nh, :], top[t][LO:LO + nh, :], SLOPE - 1.0, LIFT, ALU.mult,
                                  ALU.add).then_inc(s_small[t].sem, 1)
                dve.tensor_scalar(top2[t][LO:LO + nh, :], top[t][LO:LO + nh, :], -SLOPE, None,
                                  ALU.mult).then_inc(s_small[t].sem, 1)
                dve.wait_ge(s_small[t].sem, s_small[t].after(n, 4))
                dve.tensor_scalar(Z[t][0:nh, :], bk.t[0:nh, :], atop[t][0:nh, :], 0.0, ALU.add,
                                  ALU.max).then_inc(s_z[t].sem, 1)

            def gate_low(t, n):
                nh = heads[t]
                dve.wait_ge(s_gh[t].sem, s_gh[t].after(n, 1))
                dve.tensor_tensor(GS[t][LO:LO + nh, :], Z[t][0:nh, :], GS[t][0:nh, :].bitcast(F32),
                                  ALU.subtract).then_inc(s_gl[t].sem, 1)

            def scalars(t, n, bk, use, dst):
                w = (2 * LO if t == "a" else LO) + heads[t]
                dve.wait_ge(bk.full.sem, bk.full.after(n, use))
                dve.tensor_copy(SC[t][:], bk.t[:].rearrange("p (b w) -> p b w", b=NB)[:, :, 0:w]).then_inc(bk.free.sem, 1)
                dve.wait_ge(bk.free.sem, bk.free.after(n, use))
                if dst is not None:
                    dve.tensor_copy(dst, SC[t][:, :, 0:heads[t]]).then_inc(s_den[t].sem, 1)

            def values0(n, half):
                bk = a_o[half]
                if half == 0:
                    dve.tensor_copy(V0[:, :, :, 1, K0], SC["a"][:, :, 0:H0]).then_inc(s_den["a"].sem, 1)
                dve.wait_ge(bk.full.sem, bk.full.after(n, 1))
                for j in range(2):
                    b = 2 * half + j
                    ins = dve.tensor_tensor(V0[:, b, :, 1, 0:K0],
                                            bk.t[:, j * D:(j + 1) * D].rearrange("p (h c) -> p h c", h=H0),
                                            SC["a"][:, b, 0:H0].unsqueeze(2).to_broadcast([P, H0, K0]), ALU.mult)
                ins.then_inc(bk.free.sem, 1)
                dve.wait_ge(bk.free.sem, bk.free.after(n, 1))
                dve.wait_ge(s_den["a"].sem, s_den["a"].after(n, 1))
                for j in range(2):
                    b = 2 * half + j
                    ins = dve.tensor_tensor(V0[:, b, :, 0, :], V0[:, b, :, 1, :],
                                            SC["a"][:, b, LO:LO + H0].unsqueeze(2).to_broadcast([P, H0, C0]), ALU.mult)
                ins.then_inc(s_u.sem, 1)

            def rest(n):
                dve.wait_ge(s_hi.sem, s_hi.after(n, 2))
                if started(n):
                    dve.wait_ge(s_lo.sem, s_lo.after(n - 1, 2))
                dve.tensor_tensor(REST[:, 2:4], V0[:, 2:4], PARTS[:, 0, 2:4], ALU.subtract).then_inc(s_rest[1].sem, 1)

            def low_part(n, half):
                dve.wait_ge(s_mid.sem, s_mid.after(n, half + 1))
                b = slice(2 * half, 2 * half + 2)
                dve.tensor_tensor(PARTS[:, 2, b], REST[:, b], PARTS[:, 1, b], ALU.subtract).then_inc(s_lo.sem, 1)

            def elu(n, h):
                dve.wait_ge(s_ex.sem, s_ex.after(n, h + 1))
                dve.scalar_tensor_tensor(GT[0][:, h, :], EX, -1.0, RL, ALU.add, ALU.add).then_inc(s_el.sem, 1)
                dve.wait_ge(s_el.sem, s_el.after(n, 2 * h - 1))
                dve.scalar_tensor_tensor(EX, EX, -1.0, GT[0][:, h, :].bitcast(F32), ALU.add,
                                         ALU.subtract).then_inc(s_el.sem, 1)
                dve.wait_ge(s_el.sem, s_el.after(n, 2 * h))
                dve.tensor_tensor(GT[1][:, h, :], EX, RL, ALU.add).then_inc(s_gt.sem, 1)

            def h_low(n, k, bk):
                dve.wait_ge(s_hth.sem, s_hth.after(n, k + 1))
                dve.tensor_tensor(HT_b[1][:, k, :], bk.t[:], HT_b[0][:, k, :].bitcast(F32),
                                  ALU.subtract).then_inc(bk.free.sem, 1)

            def lonely(n):
                for bk in a_o:
                    dve.wait_ge(bk.free.sem, bk.free.after(n, 3))
                dve.tensor_scalar(none[:], MS[:, :, 0, K0], 0.0, None, ALU.is_equal).then_inc(s_none.sem, 1)

            def values1(n, b):
                bk = b_o[b % 2]
                dve.wait_ge(bk.full.sem, bk.full.after(n, 1 + b // 2))
                dve.tensor_tensor(V1[:, b, :, 0:F1], bk.t[:].rearrange("p (h c) -> p h c", h=H1),
                                  SC["b"][:, b, 0:H1].unsqueeze(2).to_broadcast([P, H1, F1]),
                                  ALU.mult).then_inc(bk.free.sem, 1)

            def weights_a(n, h):
                if h == 0:
                    dve.wait_ge(s_noedge.sem, s_noedge.after(n, 1))
                dve.wait_ge(a_g.free.sem, a_g.free.after(n, h + 2))
                if not (isinstance(n, int) and n == 0 and h < 2):
                    dve.wait_ge(s_pv["a"].sem, s_pv["a"].after(n, h - 1))
                dve.tensor_tensor(HIGH[h % 2][:], SIGN[h % 2][:], NOEDGE[:], ALU.is_gt).then_inc(s_w["a"].sem, 1)

            def weights_b(n, p, h):
                if h == 0:
                    if not started(n):
                        dve.wait_ge(folded["c"].sem, folded["c"].after(0, 2))
                    dve.wait_ge(s_diag.sem, s_diag.after(n, 2))
                s, hh = ("b", h) if h < H1 else ("c", 0)
                q = (p + h) % 2
                dve.wait_ge(b_g.free.sem, b_g.free.after(n, h + 2))
                if not (isinstance(n, int) and n == 0 and h < 2):
                    dve.wait_ge(s_pv["b"].sem, s_pv["b"].after(n, h - 1))
                for b in range(NB):
                    ins = dve.scalar_tensor_tensor(W[q][:, b, :], GB[q][:], SC[s][:, b, LO + hh:LO + hh + 1],
                                                   MASK[p][:, b, :], ALU.max, ALU.mult)
                ins.then_inc(s_w["b"].sem, 1)

            def inverse(t, n, k, src, w):
                dve.tensor_scalar(den[t][:, 0:w], src, TINY, None, ALU.max).then_inc(s_den_r[t].sem, 1)
                dve.wait_ge(s_den_r[t].sem, s_den_r[t].after(n, k))
                dve.reciprocal(rden[t][:, 0:w], den[t][:, 0:w]).then_inc(s_rden[t].sem, 1)
                dve.wait_ge(s_rden[t].sem, s_rden[t].after(n, k))

            def outputs0(n, half):
                dve.wait_ge(s_sums.sem, s_sums.after(n, 4 * half + 4))
                if half == 0:
                    dve.wait_ge(s_xm.sem, s_xm.after(n, 1))
                h = slice(4 * half, 4 * half + 4)
                sums = SUMS[:, h].rearrange("p h b c -> p (h b) c")
                inverse("a", n, half + 1, sums[:, :, K0], 4 * NB)
                dve.scalar_tensor_tensor(T[:, h].rearrange("p h b c -> p (h b) c"), sums[:, :, 0:K0], 0.0,
                                         rden["a"][:].unsqueeze(2).to_broadcast([P, 4 * NB, K0]), ALU.max,
                                         ALU.mult).then_inc(s_t.sem, 1)

            def outputs1(n, h):
                for half in range(2):
                    bk = b_o[half]
                    if half == 0:
                        dve.wait_ge(s_half.sem, s_half.after(n, h + 1))
                    else:
                        dve.wait_ge(s_pv["b"].sem, s_pv["b"].after(n, h + 1))
                    sums = bk.t[:, 0:2 * (F1 + 1)].rearrange("p (b c) -> p b c", c=F1 + 1)
                    inverse("b", n, 2 * h + half + 1, sums[:, :, F1], 2)
                    if h:
                        dve.wait_ge(b_m.full.sem, b_m.full.after(n, 3 + h))
                    dve.tensor_tensor(Y[:, 2 * half:2 * half + 2, :], sums[:, :, 0:F1],
                                      rden["b"][:, 0:2].unsqueeze(2).to_broadcast([P, 2, F1]),
                                      ALU.mult).then_inc(bk.free.sem, 1)

            def final(n, blocks):
                if blocks[0] == 0:
                    dve.wait_ge(s_x1b.sem, s_x1b.after(n, 1))
                for b in blocks:
                    bk = b_o[b % 2]
                    if b < NB - 1:
                        dve.wait_ge(s_half.sem, s_half.after(n, H1 + b + 1))
                    else:
                        dve.wait_ge(s_pv["b"].sem, s_pv["b"].after(n, H1 + 1))
                    inverse("b", n, 2 * H1 + b + 1, bk.t[:, F2:F2 + 1], 1)
                    dve.scalar_tensor_tensor(OUT[:, b, :], bk.t[:, 0:F2], rden["b"][:, 0:1], OUT[:, b, :], ALU.mult,
                                             ALU.add).then_inc(s_fin.sem, 1)

            def mask(n, p):
                dve.wait_ge(adj_in.sem, adj_in.after(n, 16))
                dve.tensor_scalar(MASK[p][:], ADJ[:], 0.0, None, ALU.is_gt).then_inc(s_mask.sem, 1)

            def no_edges(n):
                dve.wait_ge(a_m.free.sem, a_m.free.after(n, 5))
                dve.wait_ge(a_g.free.sem, a_g.free.after(n, 1))
                dve.tensor_scalar(NOEDGE[:], MASKT[:], -1.0, 1.0, ALU.mult, ALU.add).then_inc(s_noedge.sem, 1)

            def diagonal(n, p):
                dve.wait_ge(a_g.full.sem, a_g.full.after(n, 1))
                flat = MASK[p][:].rearrange("p b j -> p (b j)")
                step = N + P
                head = flat[:, 0:(NB - 1) * step].rearrange("p (b c) -> p b c", c=step)[:, :, 0:P]
                tail = flat[:, (NB - 1) * step:NB * N]
                dve.tensor_tensor(head, head, identb[:].unsqueeze(1).to_broadcast([P, NB - 1, P]),
                                  ALU.max).then_inc(s_diag.sem, 1)
                dve.tensor_tensor(tail, tail, identb[:], ALU.max).then_inc(s_diag.sem, 1)

            def joint(nb, pb, na, pa, nx, px):
                A, Bt, NX = na is not None, nb is not None, nx is not None
                if NX:
                    dve.wait_ge(x_in[px].sem, x_in[px].after(nx, 16 - 8 * px))
                    statistics("a", nx, X[px])
                if Bt:
                    gate_low("b", nb)
                    scalars("b", nb, b_m, 3, V1[:, :, :, F1])
                    values1(nb, 0)
                    values1(nb, 1)
                if A:
                    weights_a(na, 0)
                    weights_a(na, 1)
                if Bt:
                    weights_b(nb, pb, 0)
                    values1(nb, 2)
                    values1(nb, 3)
                if A:
                    lonely(na)
                if A:
                    weights_a(na, 2)
                for h in range(H1):
                    if Bt:
                        if h + 1 < H1:
                            weights_b(nb, pb, h + 1)
                        outputs1(nb, h)
                        if h >= 2:
                            elu(nb, h - 1)
                    if A:
                        weights_a(na, h + 3)
                    if NX and h == 0:
                        mean_shift("a", nx)
                    if h >= 2 and A and not Bt:
                        fold("bc"[h - 2], 0)
                        fold("bc"[h - 2], 1)
                        split_weights("bc"[h - 2])
                if A:
                    outputs0(na, 0)
                if Bt:
                    elu(nb, 3)
                if NX:
                    if not started(nx):
                        fold("a", 0)
                        fold("a", 1)
                    bounds("a", nx, a_m, 3)
                if Bt:
                    bounds("c", nb, b_m, 8)
                if A:
                    weights_a(na, 7)
                if Bt:
                    gate_low("c", nb)
                    scalars("c", nb, b_m, 9, V2[:, :, F2:F2 + 1])
                if Bt:
                    weights_b(nb, pb, H1)
                if A:
                    outputs0(na, 1)
                if NX:
                    mask(nx, px)
                    scalars("a", nx, a_m, 4, None)
                if A:
                    dve.wait_ge(s_x1.sem, s_x1.after(na, 2))
                    statistics("b", na, X1[pa])
                if Bt:
                    final(nb, (0,))
                if A:
                    mean_shift("b", na)
                if NX:
                    gate_low("a", nx)
                if NX:
                    values0(nx, 0)
                if Bt:
                    final(nb, (1,))
                if NX:
                    values0(nx, 1)
                if A:
                    h_low(na, 0, b_m)
                    h_low(na, 1, b_g)
                if Bt:
                    final(nb, (2,))
                if NX:
                    rest(nx)
                if Bt:
                    final(nb, (3,))
                if A:
                    bounds("b", na, b_m, 2)
                if NX:
                    low_part(nx, 1)
                    no_edges(nx)
                    diagonal(nx, px)

            joints(dve, joint)

        @block.tensor
        def _(pe):
            def claim(bk, n, k):
                if started(n, k):
                    pe.wait_ge(bk.free.sem, bk.free.after(n, k))

            def transpose_h(t, n, k, bk, use):
                pe.wait_ge(s_h[t].sem, s_h[t].after(n, NB))
                claim(bk, n, use)
                for b in range(NB):
                    ins = pe.transpose(bk.t[:, b * P:(b + 1) * P], Hn[t][:, b, k * P:(k + 1) * P], ident[:])
                ins.then_inc(bk.full.sem, 1)

            def score_rows(t, n, bk, use):
                claim(bk, n, use)
                if t == "a":
                    factors = [(rows_w["a"][:, k, :], HT_a[:, k, :]) for k in range(KB)]
                else:
                    high, low = HT_b if t == "b" else GT
                    factors = [pair for k in range(KB if t == "b" else FB) for pair in (
                        (rows_w_high[t][:, k, :], high[:, k, :]),
                        (rows_w_high[t][:, k, :], low[:, k, :]),
                        (rows_w_low[t][:, k, :], high[:, k, :]))]
                if not started(n):
                    done = folded["a"] if t == "a" else split_w[t]
                    pe.wait_ge(done.sem, done.after(0, done.per_batch))
                for i, (w, h) in enumerate(factors):
                    ins = pe.matmul(bk.t[0:LO + heads[t], :], w, h, start=(i == 0), stop=(i == len(factors) - 1))
                ins.then_inc(bk.full.sem, 1)

            def project(out, src, t, nk, b):
                high, low = src
                for k in range(nk):
                    hb, lb = high[:, k, b * P:(b + 1) * P], low[:, k, b * P:(b + 1) * P]
                    pe.matmul(out, hb, W_high[t][:, k, :], start=(k == 0), stop=False)
                    pe.matmul(out, hb, W_low[t][:, k, :], start=False, stop=False)
                    ins = pe.matmul(out, lb, W_high[t][:, k, :], start=False, stop=(k == nk - 1))
                return ins

            def transpose_scalars(t, n, rows_bank, rows_use, bk, use):
                pe.wait_ge(rows_bank.free.sem, rows_bank.free.after(n, rows_use))
                if t == "a":
                    pe.wait_ge(s_ga.sem, s_ga.after(n, 1))
                claim(bk, n, use)
                for b in range(NB):
                    ins = pe.transpose(bk.t[:, b * P:(b + 1) * P], RT[t][:, b * P:(b + 1) * P], ident[:])
                ins.then_inc(bk.full.sem, 1)

            def project0(n, half):
                bk = a_o[half]
                claim(bk, n, 0)
                for j in range(2):
                    b = 2 * half + j
                    for k in range(KB):
                        ins = pe.matmul(bk.t[:, j * D:(j + 1) * D], HT_a[:, k, b * P:(b + 1) * P], WP[:, k, :],
                                        start=(k == 0), stop=(k == KB - 1))
                ins.then_inc(bk.full.sem, 1)

            def project1(n, b):
                bk = b_o[b % 2]
                claim(bk, n, b // 2)
                if b < 2 and started(n):
                    pe.wait_ge(s_fin.sem, s_fin.after(n - 1, 3 + b))
                project(bk.t[:], HT_b, "b", KB, b).then_inc(bk.full.sem, 1)

            def project2(n, half):
                bk = b_o[half]
                claim(bk, n, 6)
                for j in range(2):
                    b = 2 * half + j
                    ins = project(bk.t[:, j * F2:(j + 1) * F2], GT, "c", FB, b)
                ins.then_inc(bk.full.sem, 1)

            def transpose_mask(n, p):
                pe.wait_ge(s_mask.sem, s_mask.after(n, 1))
                for half, (bk, use) in enumerate(((a_m, 4), (a_g, 0))):
                    claim(bk, n, use)
                    dst = bk.t[:].bitcast(BF16)
                    for jb in range(2):
                        j = 2 * half + jb
                        for b in range(NB):
                            ins = pe.transpose(dst[:, jb * N + b * P:jb * N + (b + 1) * P],
                                               MASK[p][:, b, j * P:(j + 1) * P], identb[:])
                    ins.then_inc(bk.full.sem, 1)

            def mean_row(n):
                claim(a_m, n, 5)
                for k in range(KB):
                    ins = pe.matmul(a_m.t[:, 0:D], hsum[:, k:k + 1].to_broadcast([P, P]), WP[:, k, :],
                                    start=(k == 0), stop=(k == KB - 1))
                ins.then_inc(a_m.full.sem, 1)

            def spread(t, n, h, bk, use):
                w = LO + heads[t]
                claim(bk, n, use)
                pe.wait_ge(s_gl[t].sem, s_gl[t].after(n, 1))
                pe.matmul(bk.t[:], pick[0:w, h:h + 1].to_broadcast([w, P]), GS[t][0:w, :], start=True, stop=True).then_inc(bk.full.sem, 1)

            def spread_a(n, h):
                spread("a", n, h, a_g, 1 + h)

            def spread_b(n, h):
                if h < H1:
                    spread("b", n, h, b_g, 1 + h)
                else:
                    spread("c", n, 0, b_g, 1 + h)

            def all_lows(n, blocks):
                if blocks[0] == 0:
                    pe.wait_ge(s_lo.sem, s_lo.after(n, 2))
                for b in blocks:
                    bk = a_o[b % 2]
                    claim(bk, n, 1 + b // 2)
                    for j in range(NB):
                        for k in range(3):
                            ins = pe.matmul(bk.t[:, 0:H0 * C0], MASKT[:, j, b * P:(b + 1) * P], PARTS[:, k, j, :, 1, :],
                                            start=(j == 0 and k == 0), stop=(j == NB - 1 and k == 2))
                    ins.then_inc(bk.full.sem, 1)

            def sums0(n, h):
                bk = a_o[h % 2]
                claim(bk, n, 3 + h // 2)
                pe.wait_ge(s_w["a"].sem, s_w["a"].after(n, h + 1))
                for b in range(NB):
                    at = b * 2 * C0
                    for j in range(NB):
                        for k in range(3):
                            ins = pe.matmul(bk.t[:, at:at + 2 * C0], HIGH[h % 2][:, j, b * P:(b + 1) * P],
                                            PARTS[:, k, j, h], start=(j == 0 and k == 0), stop=(j == NB - 1 and k == 2))
                ins.then_inc(s_pv["a"].sem, 1)

            def sums1(n, p, h):
                pe.wait_ge(s_w["b"].sem, s_w["b"].after(n, h + 1))
                if h == 0:
                    pe.wait_ge(s_den["b"].sem, s_den["b"].after(n, 1))
                    for o in b_o:
                        pe.wait_ge(o.free.sem, o.free.after(n, 2))
                for b in range(NB):
                    bk = b_o[b // 2]
                    if b % 2 == 0:
                        claim(bk, n, 2 + h)
                    at = (b % 2) * (F1 + 1)
                    for j in range(NB):
                        ins = pe.matmul(bk.t[:, at:at + F1 + 1], W[(p + h) % 2][:, j, b * P:(b + 1) * P],
                                        V1[:, j, h, :], start=(j == 0), stop=(j == NB - 1))
                    if b == 1:
                        ins.then_inc(s_half.sem, 1)
                ins.then_inc(s_pv["b"].sem, 1)

            def sums2(n, p, blocks):
                if blocks[0] == 0:
                    pe.wait_ge(s_w["b"].sem, s_w["b"].after(n, H1 + 1))
                    for o, used in zip(b_o, (7, 7)):
                        pe.wait_ge(o.free.sem, o.free.after(n, used))
                for b in blocks:
                    bk = b_o[b % 2]
                    if b >= 2:
                        pe.wait_ge(s_fin.sem, s_fin.after(n, b - 1))
                    for j in range(NB):
                        ins = pe.matmul(bk.t[:, 0:F2 + 1], W[(p + H1) % 2][:, j, b * P:(b + 1) * P], V2[:, j, :],
                                        start=(j == 0), stop=(j == NB - 1))
                    ins.then_inc(s_half.sem if b < NB - 1 else s_pv["b"].sem, 1)

            def transpose_y(n, h):
                for o in b_o:
                    pe.wait_ge(o.free.sem, o.free.after(n, 3 + h))
                claim(b_m, n, 3 + h)
                for b in range(NB):
                    ins = pe.transpose(b_m.t[:, b * P:(b + 1) * P], Y[:, b, :], ident[:])
                ins.then_inc(b_m.full.sem, 1)

            def joint(nb, pb, na, pa, nx, px):
                A, Bt, NX = na is not None, nb is not None, nx is not None
                if Bt:
                    pe.wait_ge(b_g.free.sem, b_g.free.after(nb, 1))
                    if not started(nb):
                        pe.wait_ge(wb_in.sem, wb_in.after(0, 16 * 8))
                    score_rows("b", nb, b_m, 1)
                    project1(nb, 0)
                if A:
                    mean_row(na)
                    spread_a(na, 0)
                if Bt:
                    project1(nb, 1)
                if A:
                    all_lows(na, (0, 1))
                if Bt:
                    transpose_scalars("b", nb, b_m, 2, b_m, 2)
                if A:
                    spread_a(na, 1)
                    all_lows(na, (2, 3))
                if Bt:
                    spread_b(nb, 0)
                    project1(nb, 2)
                if A:
                    spread_a(na, 2)
                    sums0(na, 0)
                if Bt:
                    project1(nb, 3)
                if A:
                    sums0(na, 1)
                for h in range(H1):
                    if Bt:
                        if h + 1 < H1:
                            spread_b(nb, h + 1)
                        if h:
                            transpose_y(nb, h - 1)
                    if A:
                        spread_a(na, h + 3)
                    if Bt:
                        sums1(nb, pb, h)
                    if A:
                        sums0(na, h + 2)
                if NX:
                    transpose_h("a", nx, 0, a_m, 0)
                if Bt:
                    transpose_y(nb, H1 - 1)
                if A:
                    spread_a(na, 7)
                if NX:
                    transpose_h("a", nx, 1, a_m, 1)
                if A:
                    sums0(na, 6)
                if NX:
                    score_rows("a", nx, a_m, 2)
                if Bt:
                    pe.wait_ge(s_gt.sem, s_gt.after(nb, H1))
                    score_rows("c", nb, b_m, 7)
                    project2(nb, 0)
                    project2(nb, 1)
                    transpose_scalars("c", nb, b_m, 8, b_m, 8)
                    spread_b(nb, H1)
                if A:
                    sums0(na, 7)
                if NX:
                    project0(nx, 0)
                    project0(nx, 1)
                    transpose_scalars("a", nx, a_m, 3, a_m, 3)
                if Bt:
                    sums2(nb, pb, (0, 1))
                if NX:
                    transpose_mask(nx, px)
                if Bt:
                    sums2(nb, pb, (2,))
                if A:
                    transpose_h("b", na, 0, b_m, 0)
                    transpose_h("b", na, 1, b_g, 0)
                if Bt:
                    sums2(nb, pb, (3,))
            pe.wait_ge(cst.sem, 11)
            pe.wait_ge(wa_in.sem, wa_in.after(0, 16 * 3))
            joints(pe, joint)


_INS = ['x', 'adj', 'L0_gnn_W_proj', 'L0_gnn_W_att', 'L0_gnn_b_att', 'L1_gnn_W1', 'L1_gnn_att_src1',
        'L1_gnn_att_dst1', 'L1_gnn_b1', 'L1_gnn_W2', 'L1_gnn_att_src2', 'L1_gnn_att_dst2', 'L1_gnn_b2']
_OUTS = [((16, 512, 256), 'float32')]


def kernel(**inputs):
    import numpy as _np
    import concourse.bacc as _bacc
    from concourse import mybir as _mybir
    from concourse.bass_utils import run_bass_kernel_spmd as _run

    nc = _bacc.Bacc("TRN2", target_bir_lowering=False, num_devices=1)
    arrays, args = {}, []
    for name in _INS:
        a = _np.ascontiguousarray(inputs[name])
        arrays[f"in_{name}_dram"] = a
        args.append(nc.dram_tensor(f"in_{name}_dram", a.shape, _mybir.dt.from_np(a.dtype), kind="ExternalInput").ap())
    for i, (shape, dtype) in enumerate(_OUTS):
        dt = _mybir.dt.from_np(_np.dtype(dtype))
        args.append(nc.dram_tensor(f"out_{i}_dram", shape, dt, kind="ExternalOutput").ap())
    gnn_kernel(nc, *args)
    r = _run(nc, [arrays], core_ids=[0])
    got = tuple(r.results[0][f"out_{i}_dram"] for i in range(len(_OUTS)))
    return got[0]
```
